# Optimizing a Trainium2 kernel written in Bass

```python
import numpy as np
import jax
import jax.numpy as jnp

def _softmax(x, axis=-1):
    return jax.nn.softmax(x, axis=axis)

def _gelu(x):
    return jax.nn.gelu(x, approximate=True)

def _silu(x):
    return jax.nn.silu(x)

def _sigmoid(x):
    return jax.nn.sigmoid(x)

def _layernorm(x, axis=-1, eps=1e-05):
    m = jnp.mean(x, axis=axis, keepdims=True)
    v = jnp.var(x, axis=axis, keepdims=True)
    return (x - m) / jnp.sqrt(v + eps)

def _scatter_add(tgt, idx, src, axis=0):
    return tgt.at[idx].add(src)

def _segment_sum(src, seg, n):
    return jax.ops.segment_sum(src, seg, n)
kernel_name = 'mk_hybrid_d1_jaxref_r4_29e3bc'

def setup_inputs(seed: int=0):
    np.random.seed(seed)
    _w = jnp.asarray

    def _L0_attn_a_setup():
        import jax, jax.numpy as jnp
        import numpy as np

        def log_g(x):
            pos = jnp.log(jnp.maximum(x, 0.0) + 0.5)
            neg = -jax.nn.softplus(-x)
            return jnp.where(x >= 0, pos, neg)

        def parallel_scan_log(log_coeffs, log_values):
            a_star = jnp.cumsum(log_coeffs, axis=1)
            log_h0_plus_b_star = jax.lax.cumlogsumexp(log_values - a_star, axis=1)
            log_h = a_star + log_h0_plus_b_star
            return jnp.exp(log_h)
        key = jax.random.key(seed)
        k1, k2 = jax.random.split(key)
        B, S, D = (8, 1024, 256)
        x = jax.random.normal(k1, (B, S, D), dtype=jnp.float32)
        W_hg = jax.random.normal(k2, (2 * D, D), dtype=jnp.float32) * (1.0 / np.sqrt(D))
        return {'x': x, 'W_hg': W_hg}
    _L0_attn_a_in = _L0_attn_a_setup()

    def _L0_attn_b_setup():
        import jax, jax.numpy as jnp
        import numpy as np
        D_MODEL, D_INNER, D_STATE = (256, 512, 16)
        BATCH, SEQ = (4, 512)

        def silu(x):
            return x * jax.nn.sigmoid(x)

        def selective_scan(u, delta, A, B, C, D):
            bsz = u.shape[0]

            def step(h, xs):
                u_t, dt_t, B_t, C_t = xs
                dA = jnp.exp(dt_t[..., None] * A)
                dBu = (dt_t * u_t)[..., None] * B_t[:, None, :]
                h = h * dA + dBu
                y_t = jnp.einsum('bds,bs->bd', h, C_t) + D * u_t
                return (h, y_t)
            h0 = jnp.zeros((bsz, u.shape[2], A.shape[1]), u.dtype)
            xs = (u.swapaxes(0, 1), delta.swapaxes(0, 1), B.swapaxes(0, 1), C.swapaxes(0, 1))
            _, ys = jax.lax.scan(step, h0, xs)
            return ys.swapaxes(0, 1)
        key = jax.random.key(seed)
        ks = jax.random.split(key, 11)
        s_in = 1.0 / np.sqrt(D_MODEL)
        s_inner = 1.0 / np.sqrt(D_INNER)
        return {'x': jax.random.normal(ks[0], (BATCH, SEQ, D_MODEL), jnp.float32), 'W_in': jax.random.normal(ks[1], (D_MODEL, 2 * D_INNER), jnp.float32) * s_in, 'b_in': jax.random.normal(ks[2], (2 * D_INNER,), jnp.float32) * s_in, 'W_xproj': jax.random.normal(ks[3], (D_INNER, 2 * D_STATE), jnp.float32) * s_inner, 'b_xproj': jax.random.normal(ks[4], (2 * D_STATE,), jnp.float32) * s_inner, 'W_dt': jax.random.normal(ks[5], (D_INNER, D_INNER), jnp.float32) * s_inner, 'b_dt': jax.random.normal(ks[6], (D_INNER,), jnp.float32) * s_inner, 'W_out': jax.random.normal(ks[7], (D_INNER, D_MODEL), jnp.float32) * s_inner, 'b_out': jax.random.normal(ks[8], (D_MODEL,), jnp.float32) * s_inner, 'A_log': jax.random.uniform(ks[9], (D_INNER, D_STATE), jnp.float32, 0.0, np.log(16.0)), 'D_param': jnp.ones((D_INNER,), jnp.float32)}
    _L0_attn_b_in = _L0_attn_b_setup()

    def _L0_ffn_setup():
        import jax, jax.numpy as jnp
        import numpy as np
        B, N, D = (4, 512, 256)
        SPARSITY = 0.01
        key = jax.random.key(seed)
        k1, k2, k3 = jax.random.split(key, 3)
        x = jax.random.normal(k1, (B, N, D), dtype=jnp.float32)
        spatial = jax.random.normal(k2, (D, D), dtype=jnp.float32) * 0.02
        freq = jnp.fft.fft(spatial, axis=-1)
        k = int(D * SPARSITY)
        mag = jnp.abs(freq)
        kth = jax.lax.top_k(mag, k)[0][:, -1:]
        w_sparse = jnp.where(mag >= kth, freq, 0.0 + 0j)
        bias = jax.random.normal(k3, (D,), dtype=jnp.float32) * 0.01
        return {'x': x, 'w_freq_real': jnp.real(w_sparse).astype(jnp.float32), 'w_freq_imag': jnp.imag(w_sparse).astype(jnp.float32), 'bias': bias}
    _L0_ffn_in = _L0_ffn_setup()
    _d = {'L0_attn_a_x': _L0_attn_a_in['x'], 'L0_attn_a_W_hg': _L0_attn_a_in['W_hg'], 'L0_attn_b_W_in': _L0_attn_b_in['W_in'], 'L0_attn_b_b_in': _L0_attn_b_in['b_in'], 'L0_attn_b_W_xproj': _L0_attn_b_in['W_xproj'], 'L0_attn_b_b_xproj': _L0_attn_b_in['b_xproj'], 'L0_attn_b_W_dt': _L0_attn_b_in['W_dt'], 'L0_attn_b_b_dt': _L0_attn_b_in['b_dt'], 'L0_attn_b_W_out': _L0_attn_b_in['W_out'], 'L0_attn_b_b_out': _L0_attn_b_in['b_out'], 'L0_attn_b_A_log': _L0_attn_b_in['A_log'], 'L0_attn_b_D_param': _L0_attn_b_in['D_param'], 'L0_ffn_w_freq_real': _L0_ffn_in['w_freq_real'], 'L0_ffn_w_freq_imag': _L0_ffn_in['w_freq_imag'], 'L0_ffn_bias': _L0_ffn_in['bias']}
    _x0 = _d['L0_attn_a_x']
    _d['L0_attn_a_x'] = jax.random.normal(jax.random.fold_in(jax.random.key(seed), 1), (16, 512, 256), dtype=_x0.dtype)
    del _x0
    return _d

def reference(L0_attn_a_x, L0_attn_a_W_hg, L0_attn_b_W_in, L0_attn_b_b_in, L0_attn_b_W_xproj, L0_attn_b_b_xproj, L0_attn_b_W_dt, L0_attn_b_b_dt, L0_attn_b_W_out, L0_attn_b_b_out, L0_attn_b_A_log, L0_attn_b_D_param, L0_ffn_w_freq_real, L0_ffn_w_freq_imag, L0_ffn_bias):

    def _L0_attn_a_ref(x, W_hg):
        import jax, jax.numpy as jnp
        import numpy as np

        def log_g(x):
            pos = jnp.log(jnp.maximum(x, 0.0) + 0.5)
            neg = -jax.nn.softplus(-x)
            return jnp.where(x >= 0, pos, neg)

        def parallel_scan_log(log_coeffs, log_values):
            a_star = jnp.cumsum(log_coeffs, axis=1)
            log_h0_plus_b_star = jax.lax.cumlogsumexp(log_values - a_star, axis=1)
            log_h = a_star + log_h0_plus_b_star
            return jnp.exp(log_h)
        hg = jnp.einsum('bsd,ed->bse', x, W_hg)
        hidden, gate = jnp.split(hg, 2, axis=-1)
        log_coeffs = -jax.nn.softplus(gate)
        log_z = -jax.nn.softplus(-gate)
        log_tilde_h = log_g(hidden)
        log_values = log_z + log_tilde_h
        out = parallel_scan_log(log_coeffs, log_values)
        return out

    def _L0_attn_b_ref(x, W_in, b_in, W_xproj, b_xproj, W_dt, b_dt, W_out, b_out, A_log, D_param):
        import jax, jax.numpy as jnp
        import numpy as np
        D_MODEL, D_INNER, D_STATE = (256, 512, 16)
        BATCH, SEQ = (4, 512)

        def silu(x):
            return x * jax.nn.sigmoid(x)

        def selective_scan(u, delta, A, B, C, D):
            bsz = u.shape[0]

            def step(h, xs):
                u_t, dt_t, B_t, C_t = xs
                dA = jnp.exp(dt_t[..., None] * A)
                dBu = (dt_t * u_t)[..., None] * B_t[:, None, :]
                h = h * dA + dBu
                y_t = jnp.einsum('bds,bs->bd', h, C_t) + D * u_t
                return (h, y_t)
            h0 = jnp.zeros((bsz, u.shape[2], A.shape[1]), u.dtype)
            xs = (u.swapaxes(0, 1), delta.swapaxes(0, 1), B.swapaxes(0, 1), C.swapaxes(0, 1))
            _, ys = jax.lax.scan(step, h0, xs)
            return ys.swapaxes(0, 1)
        xz = x @ W_in + b_in
        x_proj, z = jnp.split(xz, 2, axis=-1)
        x_conv = silu(x_proj)
        A = -jnp.exp(A_log)
        x_dbl = x_conv @ W_xproj + b_xproj
        B, C = jnp.split(x_dbl, 2, axis=-1)
        dt = jax.nn.softplus(x_conv @ W_dt + b_dt)
        y = selective_scan(x_conv, dt, A, B, C, D_param)
        y = y * silu(z)
        return y @ W_out + b_out

    def _L0_ffn_ref(x, w_freq_real, w_freq_imag, bias):
        import jax, jax.numpy as jnp
        import numpy as np
        B, N, D = (4, 512, 256)
        SPARSITY = 0.01
        w = jax.lax.complex(w_freq_real, w_freq_imag)
        x_freq = jnp.fft.fft(x, axis=-1)
        y_freq = jnp.einsum('bnd,do->bno', x_freq, w)
        y = jnp.real(jnp.fft.ifft(y_freq, axis=-1))
        return y + bias
    x = L0_attn_a_x
    x = x + _L0_attn_a_ref(_layernorm(x, axis=-1), L0_attn_a_W_hg)
    x = x + _L0_ffn_ref(_layernorm(x, axis=-1), L0_ffn_w_freq_real, L0_ffn_w_freq_imag, L0_ffn_bias)
    x = x + _L0_attn_b_ref(_layernorm(x, axis=-1), L0_attn_b_W_in, L0_attn_b_b_in, L0_attn_b_W_xproj, L0_attn_b_b_xproj, L0_attn_b_W_dt, L0_attn_b_b_dt, L0_attn_b_W_out, L0_attn_b_b_out, L0_attn_b_A_log, L0_attn_b_D_param)
    x = x + _L0_ffn_ref(_layernorm(x, axis=-1), L0_ffn_w_freq_real, L0_ffn_w_freq_imag, L0_ffn_bias)
    return x

_drawn_inputs = setup_inputs


def setup_inputs(seed=0):
    import zlib

    import numpy as np

    out = dict(_drawn_inputs(seed))
    spreads = {'L0_attn_b_D_param': (1.0, 0.2)}
    factors = {'L0_attn_b_b_dt': 8.0, 'L0_ffn_bias': 5.148}
    for name, (base, spread) in spreads.items():
        noise = np.random.default_rng([zlib.crc32(name.encode()), seed]).standard_normal(out[name].shape)
        drawn = base * np.exp(spread * noise) if base else spread * noise
        out[name] = jnp.asarray(drawn.astype(out[name].dtype))
    for name, factor in factors.items():
        out[name] = (out[name] * factor).astype(out[name].dtype)
    return out
```

```python
import concourse.bass as bass
from concourse import mybir
from contextlib import ExitStack

F32 = mybir.dt.float32
BF16 = mybir.dt.bfloat16
ALU = mybir.AluOpType
ACT = mybir.ActivationFunctionType

BATCHES, SEQ, DM = 16, 512, 256
DI, DS = 512, 16
P = 128
TT = SEQ // P
DK = DM // P
IK = DI // P
JJ = 2
UNITS = IK // JJ * DS
RING, BRING = 4, 2
EPS = 1e-5

FRONT_USES = {
    "T0": ["t00", "t01"], "GH": ["g0", "h0", "g1", "h1"], "X": ["x0", "x1"],
    "T1": ["t10", "t11"], "FF": ["f0", "f1"], "T2": ["t20", "t21"],
    "UZ": ["u0", "u1", "u2", "u3", "z0", "z1", "z2", "z3"], "XP": ["xp"],
    "DT": ["d0", "d1", "d2", "d3"],
}
BACK_USES = {"WO": ["w0", "w1"], "T3": ["t30", "t31"], "FG": ["e0", "e1"]}
BACK_AT = {0: ["Y"], 1: ["YZ"], 3: ["WO"], 4: ["S3"], 5: ["R3"], 6: ["N3"], 7: ["A3"], 8: ["T3"], 9: ["FG"]}
FRONT_AT = {2: ["S0"], 3: ["R0"], 4: ["N0"], 5: ["A0"], 6: ["T0"], 8: ["GH"], 9: ["P"], 10: ["C"],
            11: ["X"], 12: ["S1"], 13: ["R1"], 14: ["N1"], 15: ["A1"], 16: ["T1"], 17: ["FF"],
            18: ["S2"], 19: ["R2"], 20: ["N2"], 21: ["A2"], 22: ["T2"], 24: ["UZ"], 25: ["XP"],
            26: ["V"], 27: ["DT"], 28: ["SP"], 29: ["DD"]}
FRONT = [s for k in sorted(FRONT_AT) for s in FRONT_AT[k]]
BACK = [s for k in sorted(BACK_AT) for s in BACK_AT[k]]


class Batch:

    def __init__(self, r, c):
        self.r, self.c = r, c

    def count(self, per, more=0):
        n = per * self.c + more
        return n if self.r is None else self.r * (2 * per) + n

    def pair(self, per, more):
        n = per * (self.c // 2) + more
        return n if self.r is None else self.r * per + n

    def next(self, n=1):
        return Batch(self.r, self.c + n)

    @property
    def par(self):
        return self.c % 2


def shared_turns(first, front, back, last):
    order = []
    for k in range(UNITS):
        if not (last and k + 1 == UNITS):
            order += [("B", k + 1), ("C", k + 1)]
        if back:
            for s in BACK_AT.get(k, []):
                order += BACK_USES.get(s, [])
        if front:
            for s in FRONT_AT.get(k, []):
                order += FRONT_USES.get(s, [])
    return {key: first + n for n, key in enumerate(order)}


NF = sum(len(v) for v in FRONT_USES.values())
NB = sum(len(v) for v in BACK_USES.values())
STEADY = 2 * UNITS + NF + NB


class Turns:

    def __init__(self, batch):
        self.batch = batch
        c = batch.c
        if batch.r is None and c < 0:
            order = [u for s in FRONT for u in FRONT_USES.get(s, [])] + [("B", UNITS), ("C", UNITS)]
            self.at = {key: n for n, key in enumerate(order)}
        elif batch.r is None and c == 0:
            self.at = shared_turns(NF + 2, True, False, False)
        elif batch.r is None and c >= BATCHES:
            first = NF + 2 + (2 * UNITS + NF) + STEADY * (BATCHES - 2) + 2 * UNITS - 2 + NB
            self.at = {u: first + n for n, u in enumerate(u for s in BACK for u in BACK_USES.get(s, []))}
        else:
            last = batch.r is None and c == BATCHES - 1
            self.at = shared_turns(NF + 2 + 2 * UNITS + NF + STEADY * (c - 1), not last, True, last)

    def bank(self, key):
        return self.at[key] % 2

    def filled(self, key):
        return self.more(self.at[key] + 1, 2 * STEADY)

    def emptied(self, key, before=False):
        return self.more(self.at[key] // 2 + (0 if before else 1), STEADY)

    def more(self, n, per):
        return n if self.batch.r is None else self.batch.r * per + n


def build(nc, t):
    ctx = ExitStack()
    with ctx:
        def sb(name, shape, dt=F32):
            return ctx.enter_context(nc.sbuf_tensor(name, shape, dt))

        def pb(name, shape):
            return ctx.enter_context(nc.psum_tensor(name, shape, F32))

        def sem(name):
            return ctx.enter_context(nc.semaphore(name))

        whg = sb("whg", [P, DK, 2 * DM])
        mix = sb("mix", [P, DK, DM])
        win = sb("win", [P, DK, 2 * DI])
        wdt = sb("wdt", [P, IK, DI])
        wout = sb("wout", [P, IK, DM])
        wxp = sb("wxp", [P, IK, 96])
        sel = sb("sel", [96, 2 * DS, P], BF16)
        ident = sb("ident", [P, P])
        decay = sb("decay", [P, IK, DS])
        b_in = sb("b_in", [P, 2 * IK])
        b_dt = sb("b_dt", [P, IK])
        b_xp = sb("b_xp", [96, 1])
        part1 = sb("part1", [96, 1])
        part2 = sb("part2", [96, 1])
        dpar = sb("dpar", [P, IK])
        b_ff = sb("b_ff", [P, 1, DM])
        b_out = sb("b_out", [P, 1, DM])
        mhalf = sb("mhalf", [P, TT])
        xf = sb("xf", [P, TT, DM])
        xr = [sb(f"xr{i}", [P, TT, DM]) for i in range(2)]
        xn = [sb(f"xn{i}", [P, TT, DM]) for i in range(2)]
        xnT = [sb(f"xnT{i}", [P, DK, SEQ]) for i in range(2)]
        stats = [sb(f"stats{i}", [P, TT, 6]) for i in range(2)]
        mv = [sb(f"mv{i}", [P, TT, 2]) for i in range(2)]
        rs = [sb(f"rs{i}", [P, TT]) for i in range(2)]
        nm = [sb(f"nm{i}", [P, TT]) for i in range(2)]
        keep = sb("keep", [P, DK, SEQ])
        take = sb("take", [P, DK, SEQ])
        cand = sb("cand", [P, DK, SEQ])
        u = [sb(f"u{i}", [P, IK, SEQ]) for i in range(2)]
        sz = [sb(f"sz{i}", [P, IK, SEQ]) for i in range(2)]
        dt = [sb(f"dt{i}", [P, IK, SEQ]) for i in range(2)]
        dtu = [sb(f"dtu{i}", [P, IK, SEQ]) for i in range(2)]
        xd = sb("xd", [96, SEQ])
        xhi = sb("xhi", [96, SEQ], BF16)
        xlo = sb("xlo", [96, SEQ])
        xmid = sb("xmid", [96, SEQ], BF16)
        parts = [sb(f"parts{i}", [96, SEQ], BF16) for i in range(2)]
        dec = sb("dec", [P, RING, JJ, SEQ])
        Bb = sb("Bb", [P, BRING, SEQ])
        Cb = sb("Cb", [P, RING, SEQ])
        h = sb("h", [P, 2, JJ * SEQ])
        hc = sb("hc", [P, 2, JJ, SEQ])
        ys = sb("ys", [P, JJ, SEQ])
        yg = sb("yg", [P, IK, SEQ])
        fcos, fsin, fnsin, wre = (u[1][:, i, :].rearrange("p (k n) -> p k n", k=DK) for i in range(4))
        wim = dt[1][:, 0, :].rearrange("p (k n) -> p k n", k=DK)
        specP = sz[1][:, 0, :].rearrange("p (k n) -> p k n", k=DK)
        specQ = sz[1][:, 1, :].rearrange("p (k n) -> p k n", k=DK)

        drive = [pb(f"drive{i}", [P, JJ, SEQ]) for i in range(2)]
        yacc = pb("yacc", [P, JJ, SEQ])
        bank = [pb(f"bank{i}", [P, SEQ]) for i in range(2)]

        loaded = sem("loaded")
        consts = sem("consts")
        spec_full, spec_kept = sem("spec_full"), sem("spec_kept")
        mix_full, mix_kept = sem("mix_full"), sem("mix_kept")
        neg_exp, decay_ready = sem("neg_exp"), sem("decay_ready")
        filled = sem("filled")
        emptied = [sem("emptied0"), sem("emptied1")]
        x_in = [sem("x_in0"), sem("x_in1")]
        stored = [sem("stored0"), sem("stored1")]
        ln_stats, ln_mv, ln_var, ln_rs, ln_nm, ln_xn = (
            [sem(f"{n}{i}") for i in range(2)] for n in ("ln_stats", "ln_mv", "ln_var", "ln_rs", "ln_nm", "ln_xn"))
        gates, cand_neg, cand_sig, cand_in, state_a = (
            sem("gates"), sem("cand_neg"), sem("cand_sig"), sem("cand_in"), sem("state_a"))
        res_bias1, res_bias2, res_bias3 = sem("res_bias1"), sem("res_bias2"), sem("res_bias3")
        xd_ready, r1_ready, mid_ready, parts_ready = sem("xd_ready"), sem("r1_ready"), sem("mid_ready"), sem("parts_ready")
        soft_exp, soft_ln, dt_ready, dtu_ready = sem("soft_exp"), sem("soft_ln"), sem("dt_ready"), sem("dtu_ready")
        decays, driven, scanned, weighed, summed = (
            sem("decays"), sem("driven"), sem("scanned"), sem("weighed"), sem("summed"))
        y_taken, y_gated = sem("y_taken"), sem("y_gated")

        NLOAD = 0

        def wait(eng, s, n):
            if not (isinstance(n, int) and n <= 0):
                eng.wait_ge(s, n)

        def wait_emptied(eng, tn, *keys, claim=None):
            for n in range(2):
                uses = [tn.at[key] // 2 + 1 for key in keys if tn.bank(key) == n]
                if claim is not None and tn.bank(claim) == n:
                    uses.append(tn.at[claim] // 2)
                if uses:
                    wait(eng, emptied[n], tn.more(max(uses), STEADY))

        LOADS = [
            (whg[:, :, :], t["whg"].rearrange("(k p) n -> p k n", p=P)),
            (win[:, :, :], t["win"].rearrange("(k p) n -> p k n", p=P)),
            (wdt[:, :, :], t["wdt"].rearrange("(k p) n -> p k n", p=P)),
            (wout[:, :, :], t["wout"].rearrange("(k p) n -> p k n", p=P)),
            (wxp[:, :, :], t["wxp"].rearrange("(k p) n -> p k n", p=P)),
            (sel[:, :, :], t["sel"]),
            (ident[:, :], t["ident"]),
            (decay[:, :, :], t["a_log"].rearrange("(k p) n -> p k n", p=P)),
            (b_in[:, :], t["b_in"]), (b_dt[:, :], t["b_dt"]), (b_xp[:, :], t["b_xp"]),
            (part1[:, :], t["part1"]), (part2[:, :], t["part2"]), (dpar[:, :], t["dpar"]),
            (b_ff[:, 0, :], t["b_ff"].partition_broadcast(P)), (b_out[:, 0, :], t["b_out"].partition_broadcast(P)),
            (fcos, t["fcos"].rearrange("(k p) n -> p k n", p=P)),
            (fsin, t["fsin"].rearrange("(k p) n -> p k n", p=P)),
            (fnsin, t["fnsin"].rearrange("(k p) n -> p k n", p=P)),
            (wre, t["wre"].rearrange("(k p) n -> p k n", p=P)),
            (wim, t["wim"].rearrange("(k p) n -> p k n", p=P)),
        ]
        all_loaded = 16 * len(LOADS)

        block = ctx.enter_context(nc.Block())

        @block.sync
        def _(sp):
            def load_x(b):
                if b.c > 0:
                    sp.wait_ge(ln_xn[0], b.next(-1).count(3, 2))
                    sp.wait_ge(res_bias1, b.next(-1).count(1, 1))
                sp.dma_start(xf[:, :, :], t["x"][b.c].rearrange("(i p) d -> p i d", p=P)).then_inc(x_in[b.par], 16)

            def store(b, tn):
                wait_emptied(sp, tn, "e0", "e1")
                sp.dma_start(t["out"][b.c].rearrange("(i p) d -> p i d", p=P), xr[b.par][:, :, :]).then_inc(stored[b.par], 16)

            load_x(Batch(None, 0))
            for dst, src in LOADS:
                sp.dma_start(dst, src).then_inc(loaded, 16)
            load_x(Batch(None, 1))

            for c in range(BATCHES):
                if c > 0:
                    store(Batch(None, c - 1), Turns(Batch(None, c)))
                if c + 2 < BATCHES:
                    load_x(Batch(None, c + 2))
            store(Batch(None, BATCHES - 1), Turns(Batch(None, BATCHES)))
            for i in range(2):
                sp.wait_ge(stored[i], 16 * (BATCHES // 2))

        def spans(eng, prologue, scan, end):
            prologue(Turns(Batch(None, -1)))
            scan(Batch(None, 0), Turns(Batch(None, 0)))
            with eng.Fori(0, (BATCHES - 2) // 2, 1) as r:
                for c in (1, 2):
                    scan(Batch(r, c), Turns(Batch(r, c)))
            scan(Batch(None, BATCHES - 1), Turns(Batch(None, BATCHES - 1)))
            end(Turns(Batch(None, BATCHES)))

        def is_first(b):
            return b.r is None and b.c == 0

        def is_last(b):
            return b.r is None and b.c == BATCHES - 1

        def steps(front, back, b, k, tn):
            if not is_first(b):
                for s in BACK_AT.get(k, []):
                    back(s, b.next(-1), tn)
            if not is_last(b):
                for s in FRONT_AT.get(k, []):
                    front(s, b.next(), tn)

        def bc_turn(b, k, tn):
            if k > 0:
                return tn, k
            if b.r is not None and b.c == 1:
                return Turns(b), None
            return Turns(b.next(-1)), UNITS

        def wait_row(eng, b, k, tn, which):
            own, kk = bc_turn(b, k, tn)
            if kk is None:
                n = own.at[("B", 1)] - (2 if which == "B" else 1)
                n -= trailing_uses
                wait(eng, emptied[n % 2], own.more(n // 2 + 1, STEADY))
            else:
                wait(eng, emptied[own.bank((which, kk))], own.emptied((which, kk)))

        trailing_uses = sum(len(FRONT_USES.get(s, [])) for s in FRONT_AT.get(UNITS - 1, []))

        @block.scalar
        def _(act):
            act.wait_ge(loaded, all_loaded)
            act.activation(decay[:, :, :], decay[:, :, :], ACT.Exp).then_inc(neg_exp, 1)
            act.wait_ge(neg_exp, 1)
            act.activation(decay[:, :, :], decay[:, :, :], ACT.Copy, scale=-1.0).then_inc(decay_ready, 1)
            act.wait_ge(spec_full, 1)
            act.activation(specP, yacc[:, 0, :].rearrange("p (k n) -> p k n", k=DK), ACT.Copy).then_inc(spec_kept, 1)
            act.wait_ge(spec_full, 2)
            act.activation(specQ, yacc[:, 1, :].rearrange("p (k n) -> p k n", k=DK), ACT.Copy).then_inc(spec_kept, 1)
            act.wait_ge(mix_full, 1)
            act.activation(mix[:, :, :], drive[0][:, 0, :].rearrange("p (k n) -> p k n", k=DK), ACT.Copy,
                           scale=1.0 / DM).then_inc(mix_kept, 1)
            act.wait_ge(decay_ready, 1)

            def norm_rows(g, n, per, src, b):
                act.wait_ge(ln_nm[g], b.count(per, n + 1))
                for i in range(TT):
                    last = act.activation(xn[g][:, i, :], src[:, i, :], ACT.Identity,
                                          scale=rs[g][:, i:i + 1], bias=nm[g][:, i:i + 1])
                last.then_inc(ln_xn[g], 1)

            def keep_transpose(g, n, tn):
                for k in range(DK):
                    key = f"t{n}{k}"
                    act.wait_ge(filled, tn.filled(key))
                    act.activation(xnT[g][:, k, :], bank[tn.bank(key)][:, :], ACT.Copy).then_inc(emptied[tn.bank(key)], 1)

            def front(s, b, tn):
                q = b.par
                if s in ("A0", "A1", "A2"):
                    n = int(s[1])
                    norm_rows(0, n, 3, xr[q] if n == 2 else xf, b)
                elif s in ("T0", "T1", "T2"):
                    keep_transpose(0, int(s[1]), tn)
                elif s == "GH":
                    for e in range(DK):
                        g, hd = f"g{e}", f"h{e}"
                        act.wait_ge(filled, tn.filled(g))
                        act.activation(take[:, e, :], bank[tn.bank(g)][:, :], ACT.Sigmoid).then_inc(gates, 1)
                        act.activation(keep[:, e, :], bank[tn.bank(g)][:, :], ACT.Sigmoid,
                                       scale=-1.0).then_inc(emptied[tn.bank(g)], 1)
                        act.wait_ge(filled, tn.filled(hd))
                        act.activation(cand[:, e, :], bank[tn.bank(hd)][:, :], ACT.Relu, scale=-1.0).then_inc(cand_neg, 1)
                        act.wait_ge(cand_neg, b.count(DK, e + 1))
                        act.activation(cand[:, e, :], cand[:, e, :], ACT.Sigmoid, scale=-1.0).then_inc(cand_sig, 1)
                elif s == "UZ":
                    for m in range(2 * IK):
                        key = (f"u{m}" if m < IK else f"z{m - IK}")
                        dst = u[q][:, m, :] if m < IK else sz[q][:, m - IK, :]
                        act.wait_ge(filled, tn.filled(key))
                        act.activation(dst, bank[tn.bank(key)][:, :], ACT.Silu, bias=b_in[:, m:m + 1])\
                           .then_inc(emptied[tn.bank(key)], 1)
                elif s == "XP":
                    key = "xp"
                    act.wait_ge(filled, tn.filled(key))
                    act.activation(xd[:, :], bank[tn.bank(key)][0:96, :], ACT.Identity, bias=b_xp[:, :]).then_inc(xd_ready, 1)
                    act.activation(xhi[:, :], bank[tn.bank(key)][0:96, :], ACT.Identity, bias=b_xp[:, :])\
                       .then_inc(emptied[tn.bank(key)], 1)
                elif s == "V":
                    act.wait_ge(r1_ready, b.count(1, 1))
                    act.activation(xmid[:, :], xlo[:, :], ACT.Copy).then_inc(mid_ready, 1)
                elif s == "DT":
                    for m in range(IK):
                        key = f"d{m}"
                        act.wait_ge(filled, tn.filled(key))
                        act.activation(dtu[q][:, m, :], bank[tn.bank(key)][:, :], ACT.Abs, bias=b_dt[:, m:m + 1])\
                           .then_inc(soft_exp, 1)
                        act.activation(dt[q][:, m, :], bank[tn.bank(key)][:, :], ACT.Relu, bias=b_dt[:, m:m + 1])\
                           .then_inc(emptied[tn.bank(key)], 1)
                elif s == "SP":
                    act.wait_ge(soft_exp, b.count(IK + 1, IK))
                    act.activation(dtu[q][:, :, :], dtu[q][:, :, :], ACT.Exp, scale=-1.0).then_inc(soft_exp, 1)
                    act.wait_ge(soft_exp, b.count(IK + 1, IK + 1))
                    act.activation(dtu[q][:, :, :], dtu[q][:, :, :], ACT.Ln, bias=1.0).then_inc(soft_ln, 1)

            def back(s, b, tn):
                if s == "A3":
                    norm_rows(1, 0, 1, xr[b.par], b)
                elif s == "T3":
                    keep_transpose(1, 3, tn)

            def rows(b, k, tn, key):
                for which, ring, size, used in (("B", Bb, BRING, driven), ("C", Cb, RING, weighed)):
                    n = tn.bank((which, key))
                    act.wait_ge(filled, tn.filled((which, key)))
                    wait(act, used, b.count(UNITS, k - size + 1))
                    act.activation(ring[:, k % size, :], bank[n][:, :], ACT.Copy).then_inc(emptied[n], 1)

            def decay_unit(b, k):
                if k == UNITS or (is_first(b) and k == 0):
                    act.wait_ge(dt_ready, b.count(1, 2 if k == UNITS else 1))
                b, k = (b.next(), k - UNITS) if k >= UNITS else (b, k)
                wait(act, scanned, b.count(UNITS, k - RING + 1))
                for jj in range(JJ):
                    j = k // DS * JJ + jj
                    last = act.activation(dec[:, k % RING, jj, 1:SEQ], dt[b.par][:, j, 1:SEQ], ACT.Exp,
                                          scale=decay[:, j, k % DS:k % DS + 1])
                last.then_inc(decays, 1)

            def prologue(tn):
                for s in FRONT:
                    front(s, Batch(None, 0), tn)
                rows(Batch(None, -1), UNITS, tn, UNITS)
                for k in range(2):
                    decay_unit(Batch(None, 0), k)

            def scan(b, tn):
                for k in range(UNITS):
                    if not (is_last(b) and k + 1 >= UNITS):
                        rows(b, k + 1, tn, k + 1)
                    if not (is_last(b) and k + 2 >= UNITS):
                        decay_unit(b, k + 2)
                    steps(front, back, b, k, tn)

            def end(tn):
                for s in BACK:
                    back(s, Batch(None, BATCHES - 1), tn)

            spans(act, prologue, scan, end)

        @block.vector
        def _(dve):
            dve.memset(dec[:, :, :, 0:1], 0.0).then_inc(consts, 1)
            dve.memset(mhalf[:, :], -0.5).then_inc(consts, 1)
            dve.wait_ge(loaded, all_loaded)
            dve.wait_ge(consts, 2)

            def norm_stats(g, n, per, src, b):
                for i in range(TT):
                    last = dve.bn_stats(stats[g][:, i, :], src[:, i, :])
                last.then_inc(ln_stats[g], 1)
                dve.drain()
                for i in range(TT):
                    last = dve.bn_aggr(mv[g][:, i, :], stats[g][:, i, :])
                last.then_inc(ln_mv[g], 1)
                dve.wait_ge(ln_mv[g], b.count(per, n + 1))
                dve.tensor_scalar(rs[g][:, :], mv[g][:, :, 1], 1.0, EPS, ALU.mult, ALU.add).then_inc(ln_var[g], 1)

            def norm_shift(g, n, per, b):
                dve.wait_ge(ln_rs[g], b.count(per, n + 1))
                dve.scalar_tensor_tensor(nm[g][:, :], mv[g][:, :, 0], -1.0, rs[g][:, :], ALU.mult, ALU.mult)\
                   .then_inc(ln_nm[g], 1)

            def add_rows(dst, keys, tn):
                for i, key in enumerate(keys):
                    n = tn.bank(key)
                    d = dst[:, 2 * i:2 * i + 2, :]
                    dve.wait_ge(filled, tn.filled(key))
                    dve.tensor_tensor(d, d, bank[n][:, :].rearrange("p (i d) -> p i d", i=2), ALU.add)\
                       .then_inc(emptied[n], 1)

            def front(s, b, tn):
                q = b.par
                if s == "S0":
                    dve.wait_ge(x_in[q], b.pair(16, 16))
                    norm_stats(0, 0, 3, xf, b)
                elif s == "S1":
                    wait_emptied(dve, tn, "x0", "x1")
                    norm_stats(0, 1, 3, xf, b)
                elif s == "S2":
                    wait_emptied(dve, tn, "f0", "f1")
                    norm_stats(0, 2, 3, xr[q], b)
                elif s in ("N0", "N1", "N2"):
                    norm_shift(0, int(s[1]), 3, b)
                elif s == "GH":
                    for e in range(DK):
                        n = tn.bank(f"h{e}")
                        dve.wait_ge(cand_sig, b.count(DK, e + 1))
                        dve.scalar_tensor_tensor(cand[:, e, :], bank[n][:, :], 0.0, cand[:, e, :],
                                                 ALU.max, ALU.add).then_inc(emptied[n], 1)
                elif s == "C":
                    for e in range(DK):
                        dve.wait_ge(cand_in, b.count(DK, e + 1))
                        wait_emptied(dve, tn, f"g{e}")
                        dve.tensor_tensor_scan(cand[:, e, :], keep[:, e, :], take[:, e, :], 0.0,
                                               ALU.mult, ALU.add).then_inc(state_a, 1)
                elif s == "X":
                    for e in range(DK):
                        n = tn.bank(f"x{e}")
                        d = xf[:, :, e * P:(e + 1) * P]
                        dve.wait_ge(filled, tn.filled(f"x{e}"))
                        if e == 0:
                            dve.wait_ge(ln_xn[0], b.count(3, 1))
                        dve.tensor_tensor(d, d, bank[n][:, :].rearrange("p (i d) -> p i d", i=TT), ALU.add)\
                           .then_inc(emptied[n], 1)
                elif s == "FF":
                    dve.wait_ge(res_bias1, b.count(1, 1))
                    add_rows(xr[q], ("f0", "f1"), tn)
                elif s == "V":
                    dve.wait_ge(xd_ready, b.count(1, 1))
                    wait_emptied(dve, tn, "xp")
                    dve.scalar_tensor_tensor(xlo[:, :], xhi[:, :], part1[:, :], xd[:, :], ALU.mult, ALU.add)\
                       .then_inc(r1_ready, 1)
                    dve.wait_ge(mid_ready, b.count(1, 1))
                    dve.scalar_tensor_tensor(parts[q][:, :], xmid[:, :], part2[:, :], xlo[:, :], ALU.mult, ALU.add)\
                       .then_inc(parts_ready, 1)

            def take_y(b, half):
                dve.wait_ge(summed, b.count(UNITS, DS * (half + 1)))
                wait(dve, y_gated, b.count(2, half))
                for jj in range(JJ):
                    j = half * JJ + jj
                    last = dve.scalar_tensor_tensor(ys[:, jj, :], u[b.par][:, j, :], dpar[:, j:j + 1], yacc[:, jj, :],
                                                    ALU.mult, ALU.add)
                last.then_inc(y_taken, 1)

            def back(s, b, tn):
                if s == "Y":
                    take_y(b, 1)
                elif s == "WO":
                    dve.wait_ge(res_bias2, b.count(1, 1))
                    add_rows(xr[b.par], ("w0", "w1"), tn)
                elif s == "S3":
                    wait_emptied(dve, tn, "w0", "w1")
                    norm_stats(1, 0, 1, xr[b.par], b)
                elif s == "N3":
                    norm_shift(1, 0, 1, b)
                elif s == "FG":
                    dve.wait_ge(res_bias3, b.count(1, 1))
                    add_rows(xr[b.par], ("e0", "e1"), tn)

            def drive_unit(b, k, tn):
                if k == UNITS:
                    b, own, kk = b.next(), tn, UNITS
                    wait(dve, emptied[own.bank(("B", kk))], own.emptied(("B", kk)))
                    k = 0
                elif k == 0:
                    wait_row(dve, b, 0, tn, "B")
                else:
                    wait(dve, emptied[tn.bank(("B", k))], tn.emptied(("B", k)))
                if k == 0:
                    dve.wait_ge(dtu_ready, b.count(1, 1))
                wait(dve, scanned, b.count(UNITS, k - 1))
                j = k // DS * JJ
                dve.tensor_tensor(drive[k % 2][:, :, :], dtu[b.par][:, j:j + JJ, :],
                                  Bb[:, k % BRING:k % BRING + 1, :].broadcast_to((P, JJ, SEQ)), ALU.mult)\
                   .then_inc(driven, 1)

            def scan_unit(b, k):
                dve.wait_ge(decays, b.count(UNITS, k + 1))
                dve.wait_ge(driven, b.count(UNITS, k + 1))
                wait(dve, weighed, b.count(UNITS, k - 1))
                dve.tensor_tensor_scan(h[:, k % 2, :], dec[:, k % RING, :, :].rearrange("p j n -> p (j n)"),
                                       drive[k % 2][:, :, :].rearrange("p j n -> p (j n)"), 0.0,
                                       ALU.mult, ALU.add).then_inc(scanned, 1)

            def prologue(tn):
                for s in FRONT:
                    front(s, Batch(None, 0), tn)
                drive_unit(Batch(None, -1), UNITS, tn)

            def scan(b, tn):
                for k in range(UNITS):
                    if not (is_last(b) and k + 1 >= UNITS):
                        drive_unit(b, k + 1, tn)
                    scan_unit(b, k)
                    if k == DS:
                        take_y(b, 0)
                    steps(front, back, b, k, tn)

            def end(tn):
                for s in BACK:
                    back(s, Batch(None, BATCHES - 1), tn)

            spans(dve, prologue, scan, end)

        @block.gpsimd
        def _(pool):
            pool.wait_ge(loaded, all_loaded)
            pool.wait_ge(consts, 2)

            def norm_rstd(g, n, per, b):
                pool.wait_ge(ln_var[g], b.count(per, n + 1))
                pool.tensor_tensor(rs[g][:, :], rs[g][:, :], mhalf[:, :], ALU.pow).then_inc(ln_rs[g], 1)

            def wide(bias):
                return bias[:, :, :].broadcast_to((P, TT, DM))

            def front(s, b, tn):
                q = b.par
                if s in ("R0", "R1", "R2"):
                    norm_rstd(0, int(s[1]), 3, b)
                elif s == "P":
                    for e in range(DK):
                        pool.wait_ge(gates, b.count(DK, e + 1))
                        wait_emptied(pool, tn, f"h{e}")
                        pool.tensor_tensor(take[:, e, :], take[:, e, :], cand[:, e, :], ALU.mult).then_inc(cand_in, 1)
                elif s == "S1":
                    wait_emptied(pool, tn, "x0", "x1")
                    wait(pool, stored[q], b.pair(16, 0))
                    pool.tensor_tensor(xr[q][:, :, :], xf[:, :, :], wide(b_ff), ALU.add).then_inc(res_bias1, 1)
                elif s == "T2":
                    pool.wait_ge(ln_xn[0], b.count(3, 3))
                    pool.tensor_tensor(xr[q][:, :, :], xr[q][:, :, :], wide(b_out), ALU.add).then_inc(res_bias2, 1)
                elif s == "DD":
                    for m in range(0, IK, 2):
                        pool.wait_ge(soft_ln, b.count(1, 1))
                        if m == 0:
                            wait_emptied(pool, tn, "d2", "d3")
                        last = pool.tensor_tensor(dt[q][:, m:m + 2, :], dt[q][:, m:m + 2, :], dtu[q][:, m:m + 2, :], ALU.add)
                    last.then_inc(dt_ready, 1)
                    pool.wait_ge(dt_ready, b.count(1, 1))
                    for m in range(0, IK, 2):
                        last = pool.tensor_tensor(dtu[q][:, m:m + 2, :], dt[q][:, m:m + 2, :], u[q][:, m:m + 2, :], ALU.mult)
                    last.then_inc(dtu_ready, 1)

            def gate_y(b, half):
                pool.wait_ge(y_taken, b.count(2, half + 1))
                if half == 0:
                    if not is_first(b):
                        wait(pool, emptied[gate_turn["bank"]], gate_turn["n"])
                j = half * JJ
                pool.tensor_tensor(yg[:, j:j + JJ, :], ys[:, :, :], sz[b.par][:, j:j + JJ, :], ALU.mult)\
                    .then_inc(y_gated, 1)

            gate_turn = {}

            def back(s, b, tn):
                if s == "YZ":
                    gate_y(b, 1)
                elif s == "R3":
                    norm_rstd(1, 0, 1, b)
                elif s == "T3":
                    pool.wait_ge(ln_xn[1], b.count(1, 1))
                    pool.tensor_tensor(xr[b.par][:, :, :], xr[b.par][:, :, :], wide(b_ff), ALU.add).then_inc(res_bias3, 1)

            def weigh_unit(b, k, tn):
                pool.wait_ge(scanned, b.count(UNITS, k + 1))
                if k == 0:
                    wait_row(pool, b, 0, tn, "C")
                else:
                    wait(pool, emptied[tn.bank(("C", k))], tn.emptied(("C", k)))
                wait(pool, summed, b.count(UNITS, k - 1))
                pool.tensor_tensor(hc[:, k % 2, :, :], h[:, k % 2, :].rearrange("p (j n) -> p j n", j=JJ),
                                   Cb[:, k % RING:k % RING + 1, :].broadcast_to((P, JJ, SEQ)), ALU.mult)\
                    .then_inc(weighed, 1)

            def prologue(tn):
                for s in FRONT:
                    front(s, Batch(None, 0), tn)

            def scan(b, tn):
                for k in range(UNITS):
                    weigh_unit(b, k, tn)
                    if k == DS + 1:
                        if not is_first(b):
                            gate_turn["bank"], gate_turn["n"] = tn.bank("w1"), tn.emptied("w1")
                        gate_y(b, 0)
                    steps(front, back, b, k, tn)

            def end(tn):
                for s in BACK:
                    back(s, Batch(None, BATCHES - 1), tn)

            spans(pool, prologue, scan, end)

        @block.tensor
        def _(pe):
            pe.wait_ge(loaded, all_loaded)

            def mm(out, lhsT, rhs, first, last):
                return pe.matmul(out, lhsT, rhs, start=first, stop=last)

            for half, (first, second) in enumerate((((wre, fcos), (wim, fsin)), ((wim, fcos), (wre, fnsin)))):
                for n in range(DK):
                    out = yacc[:, half, n * DM:(n + 1) * DM]
                    for i, (w, f) in enumerate((first, second)):
                        for k in range(DK):
                            last = mm(out, w[:, k, n * P:(n + 1) * P], f[:, k, :], i == 0 and k == 0, i == 1 and k == DK - 1)
                last.then_inc(spec_full, 1)
            pe.wait_ge(spec_kept, 2)
            for j in range(DK):
                out = drive[0][:, 0, j * DM:(j + 1) * DM]
                for i, (s, f) in enumerate(((specP, fcos), (specQ, fnsin))):
                    for k in range(DK):
                        last = mm(out, s[:, k, j * P:(j + 1) * P], f[:, k, :], i == 0 and k == 0, i == 1 and k == DK - 1)
            last.then_inc(mix_full, 1)
            pe.wait_ge(mix_kept, 1)

            def claim(tn, key, *after):
                wait_emptied(pe, tn, *after, claim=key)
                return bank[tn.bank(key)]

            def transpose_rows(g, n, per, order, b, tn):
                pe.wait_ge(ln_xn[g], b.count(per, order + 1))
                for k in range(DK):
                    out = claim(tn, f"t{n}{k}")
                    for i in range(TT):
                        last = pe.transpose(out[:, i * P:(i + 1) * P], xn[g][:, i, k * P:(k + 1) * P], ident[:, :])
                    last.then_inc(filled, 1)

            def project(tn, key, weight, moving, n=P, after=()):
                out = claim(tn, key, *after)
                for k, (w, m) in enumerate(zip(weight, moving)):
                    last = mm(out[0:n, :], w, m, k == 0, k == len(weight) - 1)
                last.then_inc(filled, 1)

            def rows_out(tn, keys, source, weight, blocks, after=()):
                for half, key in enumerate(keys):
                    out = claim(tn, key, *after)
                    for ii in range(2):
                        i = 2 * half + ii
                        for k in range(blocks):
                            last = mm(out[:, ii * DM:(ii + 1) * DM], source[:, k, i * P:(i + 1) * P], weight[:, k, :],
                                      k == 0, k == blocks - 1)
                    last.then_inc(filled, 1)

            def front(s, b, tn):
                q = b.par
                moving = [xnT[0][:, k, :] for k in range(DK)]
                if s in ("T0", "T1", "T2"):
                    transpose_rows(0, int(s[1]), 3, int(s[1]), b, tn)
                elif s == "GH":
                    for e in range(DK):
                        for key, at in ((f"g{e}", DM + e * P), (f"h{e}", e * P)):
                            project(tn, key, [whg[:, k, at:at + P] for k in range(DK)], moving, after=("t00", "t01"))
                elif s == "X":
                    for e in range(DK):
                        pe.wait_ge(state_a, b.count(DK, e + 1))
                        out = claim(tn, f"x{e}")
                        for i in range(TT):
                            last = pe.transpose(out[:, i * P:(i + 1) * P], cand[:, e, i * P:(i + 1) * P], ident[:, :])
                        last.then_inc(filled, 1)
                elif s == "FF":
                    rows_out(tn, ("f0", "f1"), xnT[0], mix, DK, after=("t10", "t11"))
                elif s == "UZ":
                    for m in range(2 * IK):
                        project(tn, f"u{m}" if m < IK else f"z{m - IK}",
                                [win[:, k, m * P:(m + 1) * P] for k in range(DK)], moving, after=("t20", "t21"))
                elif s == "XP":
                    project(tn, "xp", [wxp[:, k, :] for k in range(IK)], [u[q][:, k, :] for k in range(IK)], 96,
                            after=[f"u{m}" for m in range(IK)])
                elif s == "DT":
                    for m in range(IK):
                        project(tn, f"d{m}", [wdt[:, k, m * P:(m + 1) * P] for k in range(IK)],
                                [u[q][:, k, :] for k in range(IK)])

            def back(s, b, tn):
                if s == "WO":
                    pe.wait_ge(y_gated, b.count(2, 2))
                    rows_out(tn, ("w0", "w1"), yg, wout, IK)
                elif s == "T3":
                    transpose_rows(1, 3, 1, 0, b, tn)
                elif s == "FG":
                    rows_out(tn, ("e0", "e1"), xnT[1], mix, DK, after=("t30", "t31"))

            def rows(b, k, tn):
                src = b.next() if k == UNITS else b
                if k == UNITS:
                    pe.wait_ge(parts_ready, src.count(1, 1))
                for which, at in (("B", 0), ("C", DS)):
                    out = claim(tn, (which, k))
                    mm(out[:, :], sel[:, at + k % DS, :], parts[src.par][:, :], True, True).then_inc(filled, 1)

            def sum_unit(b, k):
                pe.wait_ge(weighed, b.count(UNITS, k + 1))
                if k % DS == 0:
                    wait(pe, y_taken, b.count(2, k // DS))
                for jj in range(JJ):
                    last = mm(yacc[:, jj, :], ident[:, :], hc[:, k % 2, jj, :], k % DS == 0, k % DS == DS - 1)
                last.then_inc(summed, 1)

            def prologue(tn):
                for s in FRONT:
                    front(s, Batch(None, 0), tn)
                rows(Batch(None, -1), UNITS, tn)

            def scan(b, tn):
                for k in range(UNITS):
                    if not (is_last(b) and k + 1 >= UNITS):
                        rows(b, k + 1, tn)
                    if k > 0:
                        sum_unit(b, k - 1)
                    elif not is_first(b):
                        sum_unit(b.next(-1), UNITS - 1)
                    steps(front, back, b, k, tn)
                if is_last(b):
                    sum_unit(b, UNITS - 1)

            def end(tn):
                for s in BACK:
                    back(s, Batch(None, BATCHES - 1), tn)

            spans(pe, prologue, scan, end)


_OUT = (BATCHES, SEQ, DM)


def kernel(**inputs):
    import numpy as np
    import ml_dtypes
    import concourse.bacc as bacc
    from concourse.bass_utils import run_bass_kernel_spmd

    a = {k: np.asarray(v) for k, v in inputs.items()}
    phase = 2.0 * np.pi * (np.outer(np.arange(DM), np.arange(DM)) % DM) / DM
    pick = np.zeros((96, 2 * DS, P), np.float32)
    for s in range(2 * DS):
        pick[[s, 32 + s, 64 + s], s, :] = 1.0
    row = np.arange(96)[:, None]
    arrays = {
        "x": a["L0_attn_a_x"],
        "whg": a["L0_attn_a_W_hg"].T,
        "win": a["L0_attn_b_W_in"],
        "wdt": a["L0_attn_b_W_dt"],
        "wout": a["L0_attn_b_W_out"],
        "wxp": np.concatenate([a["L0_attn_b_W_xproj"]] * 3, axis=1),
        "a_log": a["L0_attn_b_A_log"],
        "b_in": a["L0_attn_b_b_in"].reshape(2 * IK, P).T,
        "b_dt": a["L0_attn_b_b_dt"].reshape(IK, P).T,
        "b_xp": np.concatenate([a["L0_attn_b_b_xproj"]] * 3).reshape(96, 1),
        "dpar": a["L0_attn_b_D_param"].reshape(IK, P).T,
        "b_ff": a["L0_ffn_bias"],
        "b_out": a["L0_attn_b_b_out"],
        "wre": a["L0_ffn_w_freq_real"],
        "wim": a["L0_ffn_w_freq_imag"],
        "fcos": np.cos(phase).astype(np.float32),
        "fsin": np.sin(phase).astype(np.float32),
        "fnsin": (-np.sin(phase)).astype(np.float32),
        "ident": np.eye(P, dtype=np.float32),
        "sel": pick.astype(ml_dtypes.bfloat16),
        "part1": np.where(row >= 32, -1.0, 0.0).astype(np.float32),
        "part2": np.where(row >= 64, -1.0, 0.0).astype(np.float32),
    }
    arrays = {k: np.ascontiguousarray(v) for k, v in arrays.items()}
    nc = bacc.Bacc("TRN2", target_bir_lowering=False, num_devices=1)
    t = {k: nc.dram_tensor("in_" + k, v.shape, mybir.dt.from_np(v.dtype), kind="ExternalInput").ap() for k, v in arrays.items()}
    t["out"] = nc.dram_tensor("out_x", _OUT, F32, kind="ExternalOutput").ap()
    build(nc, t)
    r = run_bass_kernel_spmd(nc, [{"in_" + k: v for k, v in arrays.items()}], core_ids=[0])
    return r.results[0]["out_x"]
```

```python
import concourse.bass as bass
from concourse import mybir
from contextlib import ExitStack

F32 = mybir.dt.float32
BF16 = mybir.dt.bfloat16
ALU = mybir.AluOpType
ACT = mybir.ActivationFunctionType

BATCHES, SEQ, DM = 16, 512, 256
DI, DS = 512, 16
P = 128
TT = SEQ // P
DK = DM // P
IK = DI // P
JJ = 2
UNITS = IK // JJ * DS
RING, ROWS = 4, 2
AHEAD = 2
EPS = 1e-5

FRONT_USES = {
    "T0": ["t00", "t01"], "G": ["g0", "g1"], "H": ["h0", "h1"], "X": ["x0", "x1"],
    "T1": ["t10", "t11"], "F0": ["f0"], "F1": ["f1"], "T2": ["t20", "t21"],
    "U0": ["u0", "u1"], "U1": ["u2", "u3"], "XP": ["xp"], "D0": ["d0"], "D1": ["d1"], "D2": ["d2"], "D3": ["d3"],
    "Z0": ["z0", "z1"], "Z1": ["z2", "z3"],
}
BACK_USES = {"Y0": ["y0", "y1"], "Y1": ["y2", "y3"], "W0": ["w0"], "W1": ["w1"], "T3": ["t30", "t31"],
             "E0": ["e0"], "E1": ["e1"]}
BACK_AT = {0: ["YT"], 2: ["Y0"], 3: ["Y1"], 6: ["W0"], 7: ["W1", "W0a"], 8: ["W1a", "S3"], 9: ["R3"], 10: ["A3"],
           11: ["T3"], 12: ["E0"], 13: ["E1", "E0a"], 14: ["E1a"]}
FRONT_AT = {0: ["S0"], 1: ["R0"], 2: ["A0"], 3: ["T0"], 4: ["G"], 5: ["H"], 6: ["GS"], 7: ["CD"], 8: ["C"], 9: ["Ca"],
            10: ["X"], 11: ["Xa", "S1"], 12: ["R1"], 13: ["A1"], 14: ["T1"], 15: ["F0"], 16: ["F1", "F0a"],
            17: ["F1a", "S2"], 18: ["R2"], 19: ["A2"], 20: ["T2"],
            21: ["U0"], 22: ["U1"], 23: ["SU"], 24: ["XP"], 25: ["D0", "V1"], 26: ["D1", "V2"], 27: ["D2"],
            28: ["D3"], 29: ["SP", "DD0", "Z0"], 30: ["DD1", "Z1"]}
FRONT = [s for k in sorted(FRONT_AT) for s in FRONT_AT[k]]
BACK = [s for k in sorted(BACK_AT) for s in BACK_AT[k]]
EARLY = ("R0", "R1", "R2", "R3", "C")


class Batch:

    def __init__(self, r, c):
        self.r, self.c = r, c

    def count(self, per, more=0):
        n = per * self.c + more
        return n if self.r is None else self.r * (2 * per) + n

    def pair(self, per, more):
        n = per * (self.c // 2) + more
        return n if self.r is None else self.r * per + n

    def next(self, n=1):
        return Batch(self.r, self.c + n)

    @property
    def par(self):
        return self.c % 2


def row_at(k):
    return ("B", (k + 3) // 2) if k % 2 else ("C", k // 2 + 1)


def shared_turns(first, front, back):
    order = []
    for k in range(UNITS):
        if front or row_at(k)[1] < DS:
            order.append(row_at(k))
        if back:
            for s in BACK_AT.get(k, []):
                order += BACK_USES.get(s, [])
        if front:
            for s in FRONT_AT.get(k, []):
                order += FRONT_USES.get(s, [])
    return {key: first + n for n, key in enumerate(order)}


NF = sum(len(v) for v in FRONT_USES.values())
NB = sum(len(v) for v in BACK_USES.values())
FIRST_ROWS = [("B", DS), ("C", DS), ("B", DS + 1)]
STEADY = 2 * DS + NF + NB
PROLOGUE = [u for s in FRONT for u in FRONT_USES.get(s, [])] + FIRST_ROWS
TAILS = ({key: len(PROLOGUE) - n for n, key in enumerate(PROLOGUE)},
         {key: STEADY - n for key, n in shared_turns(0, True, True).items()})


START = NF + len(FIRST_ROWS) + 2 * DS + NF


class Turns:

    def __init__(self, batch):
        self.batch = batch
        c = batch.c
        if batch.r is None and c < 0:
            self.first, order = 0, PROLOGUE
        elif batch.r is None and c >= BATCHES:
            self.first = START + STEADY * (BATCHES - 1) - NB - NF - len(FIRST_ROWS) + NB
            order = [u for s in BACK for u in BACK_USES.get(s, [])]
        else:
            first_one, last_one = batch.r is None and c == 0, batch.r is None and c == BATCHES - 1
            self.first = NF + len(FIRST_ROWS) if first_one else START + STEADY * (c - 1)
            order = shared_turns(0, not last_one, not first_one)
        self.at = {key: self.first + n for n, key in enumerate(order)}

    def before(self, key):
        tail = TAILS[self.batch.r is not None or self.batch.c > 0]
        self.at["before", key] = self.first - tail[key]
        return "before", key

    def row(self, which, s):
        return (which, s) if (which, s) in self.at else self.before((which, DS + s))

    def bank(self, key):
        return self.at[key] % 2

    def filled(self, key):
        return self.more(self.at[key] + 1, 2 * STEADY)

    def emptied(self, key, before=False):
        return self.more(self.at[key] // 2 + (0 if before else 1), STEADY)

    def more(self, n, per):
        return n if self.batch.r is None else self.batch.r * per + n


def build(nc, t):
    ctx = ExitStack()
    with ctx:
        def sb(name, shape, dt=F32):
            return ctx.enter_context(nc.sbuf_tensor(name, shape, dt))

        def pb(name, shape):
            return ctx.enter_context(nc.psum_tensor(name, shape, F32))

        def sem(name):
            return ctx.enter_context(nc.semaphore(name))

        whg = sb("whg", [P, DK, 2 * DM])
        mix = sb("mix", [P, DK, DM])
        win = sb("win", [P, DK, 2 * DI])
        wdt = sb("wdt", [P, IK, DI])
        wout = sb("wout", [P, IK, DM])
        wxp = sb("wxp", [P, IK, 96])
        sel = sb("sel", [96, 2 * DS, P], BF16)
        ident = sb("ident", [P, P])
        decay = sb("decay", [P, IK, DS])
        b_in = sb("b_in", [P, 2 * IK])
        b_dt = sb("b_dt", [P, IK])
        b_xp = sb("b_xp", [96, 1])
        part1 = sb("part1", [96, 1])
        part2 = sb("part2", [96, 1])
        dpar = sb("dpar", [P, IK])
        bias_parts = [sb(f"bias_parts{i}", [96, 2 * DM], BF16) for i in range(2)]
        mhalf = sb("mhalf", [P, TT])
        xf = sb("xf", [P, TT, DM])
        xr = [sb(f"xr{i}", [P, TT, DM]) for i in range(2)]
        xn = [sb(f"xn{i}", [P, TT, DM]) for i in range(2)]
        xnT = [sb(f"xnT{i}", [P, DK, SEQ]) for i in range(2)]
        stats = [sb(f"stats{i}", [P, TT, 6]) for i in range(2)]
        mv = [sb(f"mv{i}", [P, TT, 2]) for i in range(2)]
        rs = [sb(f"rs{i}", [P, TT]) for i in range(2)]
        nm = [sb(f"nm{i}", [P, TT]) for i in range(2)]
        keep = sb("keep", [P, DK, SEQ])
        take = sb("take", [P, DK, SEQ])
        cand = sb("cand", [P, DK, SEQ])
        u = [sb(f"u{i}", [P, IK, SEQ]) for i in range(2)]
        sz = [sb(f"sz{i}", [P, IK, SEQ]) for i in range(2)]
        dt = [sb(f"dt{i}", [P, IK, SEQ]) for i in range(2)]
        dtu = [sb(f"dtu{i}", [P, IK, SEQ]) for i in range(2)]
        xd = sb("xd", [96, SEQ])
        xhi = sb("xhi", [96, SEQ], BF16)
        xlo = sb("xlo", [96, SEQ])
        xmid = sb("xmid", [96, SEQ], BF16)
        parts = [sb(f"parts{i}", [96, SEQ], BF16) for i in range(2)]
        dec = sb("dec", [P, RING, JJ, SEQ])
        Bb = sb("Bb", [P, ROWS, SEQ])
        Cb = sb("Cb", [P, ROWS, SEQ])
        h = sb("h", [P, 2, JJ, SEQ])
        hc = sb("hc", [P, 2, JJ, SEQ])
        yT = sb("yT", [P, TT, DI])
        yg = sb("yg", [P, IK, SEQ])
        hpos = xn[0][:, :, :].rearrange("p i d -> p (i d)").rearrange("p (e n) -> p e n", e=DK)
        fcos, fsin, fnsin, wre = (u[1][:, i, :].rearrange("p (k n) -> p k n", k=DK) for i in range(4))
        wim = dt[1][:, 0, :].rearrange("p (k n) -> p k n", k=DK)
        specP = sz[1][:, 0, :].rearrange("p (k n) -> p k n", k=DK)
        specQ = sz[1][:, 1, :].rearrange("p (k n) -> p k n", k=DK)

        bias_rows = [dt[1][0:96, 1 + i, :] for i in range(2)]

        drive = [pb(f"drive{i}", [P, SEQ]) for i in range(JJ)]
        yaccT = [pb(f"yaccT{i}", [P, DI]) for i in range(TT)]
        bank = [pb(f"bank{i}", [P, SEQ]) for i in range(2)]

        loaded = sem("loaded")
        consts = sem("consts")
        spec_full, spec_kept = sem("spec_full"), sem("spec_kept")
        mix_full, mix_kept = sem("mix_full"), sem("mix_kept")
        neg_exp, decay_ready = sem("neg_exp"), sem("decay_ready")
        filled = sem("filled")
        emptied = [sem("emptied0"), sem("emptied1")]
        x_in = [sem("x_in0"), sem("x_in1")]
        stored = [sem("stored0"), sem("stored1")]
        ln_stats, ln_mv, ln_var, ln_rs, ln_nm, ln_xn = (
            [sem(f"{n}{i}") for i in range(2)] for n in ("ln_stats", "ln_mv", "ln_var", "ln_rs", "ln_nm", "ln_xn"))
        gates, cand_sig, cand_sum, cand_in, state_a = (
            sem("gates"), sem("cand_sig"), sem("cand_sum"), sem("cand_in"), sem("state_a"))
        u_ready, sz_ready = sem("u_ready"), sem("sz_ready")
        bias_hi, bias_r1, bias_mid, bias_ready = sem("bias_hi"), sem("bias_r1"), sem("bias_mid"), sem("bias_ready")
        xd_ready, r1_ready, mid_ready, parts_ready = sem("xd_ready"), sem("r1_ready"), sem("mid_ready"), sem("parts_ready")
        soft_abs, soft_exp, soft_ln, dt_ready, dtu_ready = (
            sem("soft_abs"), sem("soft_exp"), sem("soft_ln"), sem("dt_ready"), sem("dtu_ready"))
        decays, driven, scanned, weighed, summed = (
            sem("decays"), sem("driven"), sem("scanned"), sem("weighed"), sem("summed"))
        y_taken, y_gated = sem("y_taken"), sem("y_gated")

        def wait(eng, s, n):
            if not (isinstance(n, int) and n <= 0):
                eng.wait_ge(s, n)

        def wait_emptied(eng, tn, *keys, claim=None):
            for n in range(2):
                uses = [tn.at[key] // 2 + 1 for key in keys if tn.bank(key) == n]
                if claim is not None and tn.bank(claim) == n:
                    uses.append(tn.at[claim] // 2)
                if uses:
                    wait(eng, emptied[n], tn.more(max(uses), STEADY))

        LOADS = [
            (whg[:, :, :], t["whg"].rearrange("(k p) n -> p k n", p=P)),
            (win[:, :, :], t["win"].rearrange("(k p) n -> p k n", p=P)),
            (wdt[:, :, :], t["wdt"].rearrange("(k p) n -> p k n", p=P)),
            (wout[:, :, :], t["wout"].rearrange("(k p) n -> p k n", p=P)),
            (wxp[:, :, :], t["wxp"].rearrange("(k p) n -> p k n", p=P)),
            (sel[:, :, :], t["sel"]),
            (ident[:, :], t["ident"]),
            (decay[:, :, :], t["a_log"].rearrange("(k p) n -> p k n", p=P)),
            (b_in[:, :], t["b_in"]), (b_dt[:, :], t["b_dt"]), (b_xp[:, :], t["b_xp"]),
            (part1[:, :], t["part1"]), (part2[:, :], t["part2"]), (dpar[:, :], t["dpar"]),
            (bias_rows[0], t["b_ff"]), (bias_rows[1], t["b_out"]),
            (fcos, t["fcos"].rearrange("(k p) n -> p k n", p=P)),
            (fsin, t["fsin"].rearrange("(k p) n -> p k n", p=P)),
            (fnsin, t["fnsin"].rearrange("(k p) n -> p k n", p=P)),
            (wre, t["wre"].rearrange("(k p) n -> p k n", p=P)),
            (wim, t["wim"].rearrange("(k p) n -> p k n", p=P)),
        ]
        all_loaded = 16 * len(LOADS)

        block = ctx.enter_context(nc.Block())

        @block.sync
        def _(sp):
            def load_x(b):
                if b.c > 0:
                    sp.wait_ge(ln_xn[0], b.next(-1).count(3, 2))
                    wait_emptied(sp, Turns(b.next(-2)), "f0", "f1")
                sp.dma_start(xf[:, :, :], t["x"][b.c].rearrange("(i p) d -> p i d", p=P)).then_inc(x_in[b.par], 16)

            def store(b, tn):
                wait_emptied(sp, tn, "e0", "e1")
                sp.dma_start(t["out"][b.c].rearrange("(i p) d -> p i d", p=P), xr[b.par][:, :, :]).then_inc(stored[b.par], 16)

            load_x(Batch(None, 0))
            for dst, src in LOADS:
                sp.dma_start(dst, src).then_inc(loaded, 16)
            load_x(Batch(None, 1))

            for c in range(BATCHES):
                if c > 0:
                    store(Batch(None, c - 1), Turns(Batch(None, c)))
                if c + 2 < BATCHES:
                    load_x(Batch(None, c + 2))
            store(Batch(None, BATCHES - 1), Turns(Batch(None, BATCHES)))
            for i in range(2):
                sp.wait_ge(stored[i], 16 * (BATCHES // 2))

        def spans(eng, prologue, scan, end):
            prologue(Turns(Batch(None, -1)))
            scan(Batch(None, 0), Turns(Batch(None, 0)))
            with eng.Fori(0, (BATCHES - 2) // 2, 1) as r:
                for c in (1, 2):
                    scan(Batch(r, c), Turns(Batch(r, c)))
            scan(Batch(None, BATCHES - 1), Turns(Batch(None, BATCHES - 1)))
            end(Turns(Batch(None, BATCHES)))

        def is_first(b):
            return b.r is None and b.c == 0

        def is_last(b):
            return b.r is None and b.c == BATCHES - 1

        def steps(front, back, b, k, tn, only=FRONT + BACK):
            if not is_first(b):
                for s in BACK_AT.get(k, []):
                    if s in only:
                        back(s, b.next(-1), tn)
            if not is_last(b):
                for s in FRONT_AT.get(k, []):
                    if s in only:
                        front(s, b.next(), tn)

        def wait_row(eng, tn, which, s):
            wait_emptied(eng, tn, tn.row(which, s))

        @block.scalar
        def _(act):
            act.wait_ge(loaded, all_loaded)
            act.activation(decay[:, :, :], decay[:, :, :], ACT.Exp).then_inc(neg_exp, 1)
            act.wait_ge(neg_exp, 1)
            act.activation(decay[:, :, :], decay[:, :, :], ACT.Copy, scale=-1.0).then_inc(decay_ready, 1)
            act.wait_ge(spec_full, 1)
            act.activation(specP, yaccT[0][:, :].rearrange("p (k n) -> p k n", k=DK), ACT.Copy).then_inc(spec_kept, 1)
            act.wait_ge(spec_full, 2)
            act.activation(specQ, yaccT[1][:, :].rearrange("p (k n) -> p k n", k=DK), ACT.Copy).then_inc(spec_kept, 1)
            act.wait_ge(mix_full, 1)
            act.activation(mix[:, :, :], drive[0][:, :].rearrange("p (k n) -> p k n", k=DK), ACT.Copy,
                           scale=1.0 / DM).then_inc(mix_kept, 1)
            act.wait_ge(decay_ready, 1)
            for i in range(2):
                wait(act, bias_ready, i)
                act.activation(xhi[:, :], bias_rows[i], ACT.Copy).then_inc(bias_hi, 1)
                act.wait_ge(bias_r1, i + 1)
                act.activation(xmid[:, :], xlo[:, :], ACT.Copy).then_inc(bias_mid, 1)
            act.wait_ge(bias_ready, 2)

            def norm_rows(g, n, per, src, b):
                act.wait_ge(ln_nm[g], b.count(per, n + 1))
                for i in range(TT):
                    last = act.activation(xn[g][:, i, :], src[:, i, :], ACT.Identity,
                                          scale=rs[g][:, i:i + 1], bias=nm[g][:, i:i + 1])
                last.then_inc(ln_xn[g], 1)

            def keep_transpose(g, n, tn):
                for k in range(DK):
                    key = f"t{n}{k}"
                    act.wait_ge(filled, tn.filled(key))
                    act.activation(xnT[g][:, k, :], bank[tn.bank(key)][:, :], ACT.Copy).then_inc(emptied[tn.bank(key)], 1)

            def front(s, b, tn):
                q = b.par
                if s in ("A0", "A1", "A2"):
                    n = int(s[1])
                    norm_rows(0, n, 3, xr[q] if n == 2 else xf, b)
                elif s in ("T0", "T1", "T2"):
                    keep_transpose(0, int(s[1]), tn)
                elif s == "G":
                    for e in range(DK):
                        n = tn.bank(f"g{e}")
                        act.wait_ge(filled, tn.filled(f"g{e}"))
                        act.activation(take[:, e, :], bank[n][:, :], ACT.Copy).then_inc(emptied[n], 1)
                elif s == "H":
                    for e in range(DK):
                        n = tn.bank(f"h{e}")
                        act.wait_ge(filled, tn.filled(f"h{e}"))
                        act.activation(cand[:, e, :], bank[n][:, :], ACT.Relu, scale=-1.0)
                        act.activation(hpos[:, e, :], bank[n][:, :], ACT.Relu).then_inc(emptied[n], 1)
                elif s == "GS":
                    wait_emptied(act, tn, "g0", "g1", "h0", "h1")
                    act.activation(cand[:, :, :], cand[:, :, :], ACT.Sigmoid, scale=-1.0).then_inc(cand_sig, 1)
                    act.activation(keep[:, :, :], take[:, :, :], ACT.Sigmoid, scale=-1.0).then_inc(gates, 1)
                    act.wait_ge(gates, b.count(2, 1))
                    act.activation(take[:, :, :], take[:, :, :], ACT.Sigmoid).then_inc(gates, 1)
                elif s in ("U0", "U1", "Z0", "Z1"):
                    for m in (2 * int(s[1]), 2 * int(s[1]) + 1):
                        key = s[0].lower() + str(m)
                        dst, at = (u[q], m) if s[0] == "U" else (sz[q], IK + m)
                        act.wait_ge(filled, tn.filled(key))
                        act.activation(dst[:, m, :], bank[tn.bank(key)][:, :], ACT.Identity, bias=b_in[:, at:at + 1])\
                           .then_inc(emptied[tn.bank(key)], 1)
                elif s == "SU":
                    wait_emptied(act, tn, "u0", "u1", "u2", "u3")
                    act.activation(u[q][:, :, :], u[q][:, :, :], ACT.Silu).then_inc(u_ready, 1)
                elif s == "XP":
                    key = "xp"
                    act.wait_ge(filled, tn.filled(key))
                    act.activation(xd[:, :], bank[tn.bank(key)][0:96, :], ACT.Identity, bias=b_xp[:, :]).then_inc(xd_ready, 1)
                    act.activation(xhi[:, :], bank[tn.bank(key)][0:96, :], ACT.Identity, bias=b_xp[:, :])\
                       .then_inc(emptied[tn.bank(key)], 1)
                elif s == "V2":
                    act.wait_ge(r1_ready, b.count(1, 1))
                    act.activation(xmid[:, :], xlo[:, :], ACT.Copy).then_inc(mid_ready, 1)
                elif s in ("D0", "D1", "D2", "D3"):
                    m, key = int(s[1]), s.lower()
                    act.wait_ge(filled, tn.filled(key))
                    act.activation(dtu[q][:, m, :], bank[tn.bank(key)][:, :], ACT.Abs, bias=b_dt[:, m:m + 1])\
                       .then_inc(soft_abs, 1)
                    act.activation(dt[q][:, m, :], bank[tn.bank(key)][:, :], ACT.Relu, bias=b_dt[:, m:m + 1])\
                       .then_inc(emptied[tn.bank(key)], 1)
                elif s == "SP":
                    v = dtu[q][:, :, :]
                    act.wait_ge(soft_abs, b.count(IK, IK))
                    act.activation(v, v, ACT.Exp, scale=-1.0).then_inc(soft_exp, 1)
                    act.wait_ge(soft_exp, b.count(1, 1))
                    act.activation(v, v, ACT.Ln, bias=1.0).then_inc(soft_ln, 1)

            def back(s, b, tn):
                if s == "YT":
                    act.wait_ge(summed, b.count(UNITS, UNITS))
                    for i in range(TT):
                        act.activation(yT[:, i, :], yaccT[i][:, :], ACT.Copy).then_inc(y_taken, 1)
                elif s == "A3":
                    norm_rows(1, 0, 1, xr[b.par], b)
                elif s == "T3":
                    keep_transpose(1, 3, tn)

            def copy_row(b, key, tn):
                which, s = key
                ring, used = (Bb, driven) if which == "B" else (Cb, weighed)
                per = UNITS * JJ if which == "B" else UNITS
                n = tn.bank(key)
                act.wait_ge(filled, tn.filled(key))
                wait(act, used, b.count(per, (s - ROWS + 1) * (per // DS)))
                act.activation(ring[:, s % ROWS, :], bank[n][:, :], ACT.Copy).then_inc(emptied[n], 1)

            def decay_unit(b, k):
                b, k = (b.next(), k - UNITS) if k >= UNITS else (b, k)
                if k < JJ:
                    act.wait_ge(dt_ready, b.count(2, k + 1))
                wait(act, scanned, b.count(UNITS * JJ, (k - RING + 1) * JJ))
                for jj in range(JJ):
                    s, j = k // JJ, k % JJ * JJ + jj
                    last = act.activation(dec[:, k % RING, jj, 1:SEQ], dt[b.par][:, j, 1:SEQ], ACT.Exp,
                                          scale=decay[:, j, s:s + 1])
                last.then_inc(decays, 1)

            def prologue(tn):
                for s in FRONT:
                    front(s, Batch(None, 0), tn)
                for key in FIRST_ROWS:
                    copy_row(Batch(None, -1), key, tn)
                for k in range(AHEAD):
                    decay_unit(Batch(None, 0), k)

            def scan(b, tn):
                for k in range(UNITS):
                    if row_at(k) in tn.at:
                        copy_row(b, row_at(k), tn)
                    if not (is_last(b) and k + AHEAD >= UNITS):
                        decay_unit(b, k + AHEAD)
                    steps(front, back, b, k, tn)
                    if "SU" in FRONT_AT.get(k, []):
                        wait_emptied(act, tn, *(tn.before(f"z{m}") for m in range(IK)))
                        act.activation(sz[b.par][:, :, :], sz[b.par][:, :, :], ACT.Silu).then_inc(sz_ready, 1)

            def end(tn):
                for s in BACK:
                    back(s, Batch(None, BATCHES - 1), tn)

            spans(act, prologue, scan, end)

        @block.vector
        def _(dve):
            dve.memset(dec[:, :, :, 0:1], 0.0).then_inc(consts, 1)
            dve.memset(mhalf[:, :], -0.5).then_inc(consts, 1)
            dve.wait_ge(loaded, all_loaded)
            dve.wait_ge(consts, 2)
            for i in range(2):
                dve.wait_ge(bias_hi, i + 1)
                dve.scalar_tensor_tensor(xlo[:, :], xhi[:, :], part1[:, :], bias_rows[i], ALU.mult, ALU.add).then_inc(bias_r1, 1)
                dve.wait_ge(bias_mid, i + 1)
                dve.scalar_tensor_tensor(bias_parts[i][:, :], xmid[:, :], part2[:, :], xlo[:, :], ALU.mult, ALU.add)\
                   .then_inc(bias_ready, 1)

            def norm_stats(g, n, per, src, b):
                for i in range(TT):
                    last = dve.bn_stats(stats[g][:, i, :], src[:, i, :])
                last.then_inc(ln_stats[g], 1)
                dve.drain()
                for i in range(TT):
                    last = dve.bn_aggr(mv[g][:, i, :], stats[g][:, i, :])
                last.then_inc(ln_mv[g], 1)
                dve.wait_ge(ln_mv[g], b.count(per, n + 1))
                dve.tensor_scalar(rs[g][:, :], mv[g][:, :, 1], 1.0, EPS, ALU.mult, ALU.add).then_inc(ln_var[g], 1)

            def norm_shift(g, n, per, b):
                dve.wait_ge(ln_rs[g], b.count(per, n + 1))
                dve.scalar_tensor_tensor(nm[g][:, :], mv[g][:, :, 0], -1.0, rs[g][:, :], ALU.mult, ALU.mult)\
                   .then_inc(ln_nm[g], 1)

            def add_rows(dst, src, key, tn):
                n, i = tn.bank(key), int(key[1])
                at = slice(2 * i, 2 * i + 2)
                dve.wait_ge(filled, tn.filled(key))
                dve.tensor_tensor(dst[:, at, :], src[:, at, :], bank[n][:, :].rearrange("p (i d) -> p i d", i=2), ALU.add)\
                   .then_inc(emptied[n], 1)

            def front(s, b, tn):
                q = b.par
                if s == "S0":
                    dve.wait_ge(x_in[q], b.pair(16, 16))
                    norm_stats(0, 0, 3, xf, b)
                elif s == "S1":
                    wait_emptied(dve, tn, "x0", "x1")
                    norm_stats(0, 1, 3, xf, b)
                elif s == "S2":
                    wait_emptied(dve, tn, "f0", "f1")
                    norm_stats(0, 2, 3, xr[q], b)
                elif s in ("R0", "R1", "R2"):
                    norm_shift(0, int(s[1]), 3, b)
                elif s == "CD":
                    dve.wait_ge(cand_sig, b.count(1, 1))
                    wait_emptied(dve, tn, "h0", "h1")
                    dve.tensor_tensor(cand[:, :, :], hpos, cand[:, :, :], ALU.add).then_inc(cand_sum, 1)
                elif s == "Ca":
                    for e in range(DK):
                        dve.wait_ge(cand_in, b.count(DK, e + 1))
                        dve.tensor_tensor_scan(cand[:, e, :], keep[:, e, :], take[:, e, :], 0.0,
                                               ALU.mult, ALU.add).then_inc(state_a, 1)
                elif s == "Xa":
                    for e in range(DK):
                        n = tn.bank(f"x{e}")
                        d = xf[:, :, e * P:(e + 1) * P]
                        dve.wait_ge(filled, tn.filled(f"x{e}"))
                        if e == 0:
                            dve.wait_ge(ln_xn[0], b.count(3, 1))
                        dve.tensor_tensor(d, d, bank[n][:, :].rearrange("p (i d) -> p i d", i=TT), ALU.add)\
                           .then_inc(emptied[n], 1)
                elif s in ("F0a", "F1a"):
                    wait(dve, stored[q], b.pair(16, 0))
                    add_rows(xr[q], xf, "f" + s[1], tn)
                elif s == "V1":
                    dve.wait_ge(xd_ready, b.count(1, 1))
                    wait_emptied(dve, tn, "xp")
                    dve.scalar_tensor_tensor(xlo[:, :], xhi[:, :], part1[:, :], xd[:, :], ALU.mult, ALU.add)\
                       .then_inc(r1_ready, 1)
                elif s == "V2":
                    dve.wait_ge(mid_ready, b.count(1, 1))
                    dve.scalar_tensor_tensor(parts[q][:, :], xmid[:, :], part2[:, :], xlo[:, :], ALU.mult, ALU.add)\
                       .then_inc(parts_ready, 1)

            def back(s, b, tn):
                if s in ("Y0", "Y1"):
                    for j in (2 * int(s[1]), 2 * int(s[1]) + 1):
                        n = tn.bank(f"y{j}")
                        dve.wait_ge(filled, tn.filled(f"y{j}"))
                        dve.scalar_tensor_tensor(yg[:, j, :], u[b.par][:, j, :], dpar[:, j:j + 1], bank[n][:, :],
                                                 ALU.mult, ALU.add).then_inc(emptied[n], 1)
                elif s in ("W0a", "W1a", "E0a", "E1a"):
                    add_rows(xr[b.par], xr[b.par], s[0:2].lower(), tn)
                elif s == "S3":
                    wait_emptied(dve, tn, "w0", "w1")
                    norm_stats(1, 0, 1, xr[b.par], b)
                elif s == "R3":
                    norm_shift(1, 0, 1, b)

            def drive_unit(b, k, tn):
                key = tn.row("B", k // JJ)
                b, k = (b.next(), k - UNITS) if k >= UNITS else (b, k)
                wait_emptied(dve, tn, key)
                if k < JJ:
                    dve.wait_ge(dtu_ready, b.count(2, k + 1))
                s = k // JJ
                for jj in range(JJ):
                    wait(dve, scanned, b.count(UNITS * JJ, (k - 1) * JJ + jj + 1))
                    dve.tensor_tensor(drive[jj][:, :], dtu[b.par][:, k % JJ * JJ + jj, :], Bb[:, s % ROWS, :], ALU.mult)\
                       .then_inc(driven, 1)

            def scan_unit(b, k):
                dve.wait_ge(decays, b.count(UNITS, k + 1))
                wait(dve, weighed, b.count(UNITS, k - 1))
                for jj in range(JJ):
                    dve.wait_ge(driven, b.count(UNITS * JJ, k * JJ + jj + 1))
                    dve.tensor_tensor_scan(h[:, k % 2, jj, :], dec[:, k % RING, jj, :], drive[jj][:, :], 0.0,
                                           ALU.mult, ALU.add).then_inc(scanned, 1)

            def prologue(tn):
                for s in FRONT:
                    front(s, Batch(None, 0), tn)
                drive_unit(Batch(None, -1), UNITS, tn)

            def scan(b, tn):
                for k in range(UNITS):
                    scan_unit(b, k)
                    if not (is_last(b) and k + 1 >= UNITS):
                        drive_unit(b, k + 1, tn)
                    steps(front, back, b, k, tn)

            def end(tn):
                for s in BACK:
                    back(s, Batch(None, BATCHES - 1), tn)

            spans(dve, prologue, scan, end)

        @block.gpsimd
        def _(pool):
            pool.wait_ge(loaded, all_loaded)
            pool.wait_ge(consts, 2)

            def norm_rstd(g, n, per, b):
                pool.wait_ge(ln_var[g], b.count(per, n + 1))
                pool.tensor_tensor(rs[g][:, :], rs[g][:, :], mhalf[:, :], ALU.pow).then_inc(ln_rs[g], 1)

            def front(s, b, tn):
                q = b.par
                if s in ("R0", "R1", "R2"):
                    norm_rstd(0, int(s[1]), 3, b)
                elif s == "C":
                    for e in range(DK):
                        pool.wait_ge(gates, b.count(2, 2))
                        pool.wait_ge(cand_sum, b.count(1, 1))
                        pool.tensor_tensor(take[:, e, :], take[:, e, :], cand[:, e, :], ALU.mult).then_inc(cand_in, 1)
                elif s in ("DD0", "DD1"):
                    half = int(s[2])
                    at = slice(JJ * half, JJ * half + JJ)
                    pool.wait_ge(soft_ln, b.count(1, 1))
                    wait_emptied(pool, tn, f"d{JJ * half}", f"d{JJ * half + 1}")
                    pool.tensor_tensor(dt[q][:, at, :], dt[q][:, at, :], dtu[q][:, at, :], ALU.add).then_inc(dt_ready, 1)
                    pool.wait_ge(dt_ready, b.count(2, half + 1))
                    pool.wait_ge(u_ready, b.count(1, 1))
                    pool.tensor_tensor(dtu[q][:, at, :], dt[q][:, at, :], u[q][:, at, :], ALU.mult).then_inc(dtu_ready, 1)

            def back(s, b, tn):
                if s in ("Y0", "Y1"):
                    half = int(s[1])
                    at = slice(JJ * half, JJ * half + JJ)
                    wait_emptied(pool, tn, f"y{JJ * half}", f"y{JJ * half + 1}")
                    pool.wait_ge(sz_ready, b.count(1, 1))
                    pool.tensor_tensor(yg[:, at, :], yg[:, at, :], sz[b.par][:, at, :], ALU.mult).then_inc(y_gated, 1)
                elif s == "R3":
                    norm_rstd(1, 0, 1, b)

            def weigh_unit(b, k, tn):
                pool.wait_ge(scanned, b.count(UNITS * JJ, (k + 1) * JJ))
                s = k // JJ
                wait_row(pool, tn, "C", s)
                wait(pool, summed, b.count(UNITS, k - 1))
                pool.tensor_tensor(hc[:, k % 2, :, :], h[:, k % 2, :, :],
                                   Cb[:, s % ROWS:s % ROWS + 1, :].broadcast_to((P, JJ, SEQ)), ALU.mult)\
                    .then_inc(weighed, 1)

            def prologue(tn):
                for s in FRONT:
                    front(s, Batch(None, 0), tn)

            def early(s):
                return s in EARLY

            def scan(b, tn):
                for k in range(UNITS):
                    steps(front, back, b, k, tn, [s for s in FRONT + BACK if early(s)])
                    weigh_unit(b, k, tn)
                    steps(front, back, b, k, tn, [s for s in FRONT + BACK if not early(s)])

            def end(tn):
                for s in BACK:
                    back(s, Batch(None, BATCHES - 1), tn)

            spans(pool, prologue, scan, end)

        @block.tensor
        def _(pe):
            pe.wait_ge(loaded, all_loaded)

            def mm(out, lhsT, rhs, first, last):
                return pe.matmul(out, lhsT, rhs, start=first, stop=last)

            for half, (first, second) in enumerate((((wre, fcos), (wim, fsin)), ((wim, fcos), (wre, fnsin)))):
                for n in range(DK):
                    out = yaccT[half][:, n * DM:(n + 1) * DM]
                    for i, (w, f) in enumerate((first, second)):
                        for k in range(DK):
                            last = mm(out, w[:, k, n * P:(n + 1) * P], f[:, k, :], i == 0 and k == 0, i == 1 and k == DK - 1)
                last.then_inc(spec_full, 1)
            pe.wait_ge(spec_kept, 2)
            for j in range(DK):
                out = drive[0][:, j * DM:(j + 1) * DM]
                for i, (s, f) in enumerate(((specP, fcos), (specQ, fnsin))):
                    for k in range(DK):
                        last = mm(out, s[:, k, j * P:(j + 1) * P], f[:, k, :], i == 0 and k == 0, i == 1 and k == DK - 1)
            last.then_inc(mix_full, 1)
            pe.wait_ge(mix_kept, 1)

            def claim(tn, key, *after):
                wait_emptied(pe, tn, *after, claim=key)
                return bank[tn.bank(key)]

            def transpose_rows(g, n, per, order, b, tn):
                pe.wait_ge(ln_xn[g], b.count(per, order + 1))
                for k in range(DK):
                    out = claim(tn, f"t{n}{k}")
                    for i in range(TT):
                        last = pe.transpose(out[:, i * P:(i + 1) * P], xn[g][:, i, k * P:(k + 1) * P], ident[:, :])
                    last.then_inc(filled, 1)

            def project(tn, key, weight, moving, n=P, after=()):
                out = claim(tn, key, *after)
                for k, (w, m) in enumerate(zip(weight, moving)):
                    last = mm(out[0:n, :], w, m, k == 0, k == len(weight) - 1)
                last.then_inc(filled, 1)

            def rows_out(tn, key, source, weight, blocks, bias, after=()):
                out = claim(tn, key, *after)
                mm(out[:, :], sel[:, 0, :], bias[:, :], True, False)
                for ii in range(2):
                    i = 2 * int(key[1]) + ii
                    for k in range(blocks):
                        last = mm(out[:, ii * DM:(ii + 1) * DM], source[:, k, i * P:(i + 1) * P], weight[:, k, :],
                                  False, ii == 1 and k == blocks - 1)
                last.then_inc(filled, 1)

            def front(s, b, tn):
                q = b.par
                moving = [xnT[0][:, k, :] for k in range(DK)]
                if s in ("T0", "T1", "T2"):
                    transpose_rows(0, int(s[1]), 3, int(s[1]), b, tn)
                elif s in ("G", "H"):
                    for e in range(DK):
                        at = (DM if s == "G" else 0) + e * P
                        project(tn, s.lower() + str(e), [whg[:, k, at:at + P] for k in range(DK)], moving, after=("t00", "t01"))
                elif s == "X":
                    for e in range(DK):
                        pe.wait_ge(state_a, b.count(DK, e + 1))
                        out = claim(tn, f"x{e}")
                        for i in range(TT):
                            last = pe.transpose(out[:, i * P:(i + 1) * P], cand[:, e, i * P:(i + 1) * P], ident[:, :])
                        last.then_inc(filled, 1)
                elif s in ("F0", "F1"):
                    rows_out(tn, s.lower(), xnT[0], mix, DK, bias_parts[0], after=("t10", "t11"))
                elif s in ("U0", "U1", "Z0", "Z1"):
                    for m in (2 * int(s[1]), 2 * int(s[1]) + 1):
                        at = (0 if s[0] == "U" else DI) + m * P
                        project(tn, s[0].lower() + str(m), [win[:, k, at:at + P] for k in range(DK)], moving,
                                after=("t20", "t21"))
                elif s == "XP":
                    pe.wait_ge(u_ready, b.count(1, 1))
                    project(tn, "xp", [wxp[:, k, :] for k in range(IK)], [u[q][:, k, :] for k in range(IK)], 96)
                elif s in ("D0", "D1", "D2", "D3"):
                    m = int(s[1])
                    project(tn, s.lower(), [wdt[:, k, m * P:(m + 1) * P] for k in range(IK)],
                            [u[q][:, k, :] for k in range(IK)])

            def back(s, b, tn):
                if s in ("Y0", "Y1"):
                    pe.wait_ge(y_taken, b.count(TT, TT))
                    for j in (2 * int(s[1]), 2 * int(s[1]) + 1):
                        out = claim(tn, f"y{j}")
                        for i in range(TT):
                            last = pe.transpose(out[:, i * P:(i + 1) * P], yT[:, i, j * P:(j + 1) * P], ident[:, :])
                        last.then_inc(filled, 1)
                elif s in ("W0", "W1"):
                    pe.wait_ge(y_gated, b.count(2, 2))
                    rows_out(tn, s.lower(), yg, wout, IK, bias_parts[1])
                elif s == "T3":
                    transpose_rows(1, 3, 1, 0, b, tn)
                elif s in ("E0", "E1"):
                    rows_out(tn, s.lower(), xnT[1], mix, DK, bias_parts[0], after=("t30", "t31"))

            def send_row(b, key, tn):
                which, s = key
                src = b.next() if s >= DS else b
                if s >= DS:
                    pe.wait_ge(parts_ready, src.count(1, 1))
                out = claim(tn, key)
                mm(out[:, :], sel[:, (DS if which == "C" else 0) + s % DS, :], parts[src.par][:, :], True, True)\
                    .then_inc(filled, 1)

            def sum_unit(b, k):
                pe.wait_ge(weighed, b.count(UNITS, k + 1))
                if k == 0:
                    wait(pe, y_taken, b.count(TT, 0))
                for jj in range(JJ):
                    j = k % JJ * JJ + jj
                    for i in range(TT):
                        last = pe.matmul(yaccT[i][:, j * P:(j + 1) * P], hc[:, k % 2, jj, i * P:(i + 1) * P], ident[:, :],
                                         start=k == 0 and jj == 0, stop=k == UNITS - 1 and jj == JJ - 1,
                                         is_transpose=True, skip_group_check=True)
                last.then_inc(summed, 1)

            def prologue(tn):
                for s in FRONT:
                    front(s, Batch(None, 0), tn)
                for key in FIRST_ROWS:
                    send_row(Batch(None, -1), key, tn)

            def scan(b, tn):
                for k in range(UNITS):
                    if row_at(k) in tn.at:
                        send_row(b, row_at(k), tn)
                    if k > 0:
                        sum_unit(b, k - 1)
                    elif not is_first(b):
                        sum_unit(b.next(-1), UNITS - 1)
                    steps(front, back, b, k, tn)
                if is_last(b):
                    sum_unit(b, UNITS - 1)

            def end(tn):
                for s in BACK:
                    back(s, Batch(None, BATCHES - 1), tn)

            spans(pe, prologue, scan, end)


_OUT = (BATCHES, SEQ, DM)


def kernel(**inputs):
    import numpy as np
    import ml_dtypes
    import concourse.bacc as bacc
    from concourse.bass_utils import run_bass_kernel_spmd

    a = {k: np.asarray(v) for k, v in inputs.items()}
    phase = 2.0 * np.pi * (np.outer(np.arange(DM), np.arange(DM)) % DM) / DM
    pick = np.zeros((96, 2 * DS, P), np.float32)
    for s in range(2 * DS):
        pick[[s, 32 + s, 64 + s], s, :] = 1.0
    row = np.arange(96)[:, None]
    arrays = {
        "x": a["L0_attn_a_x"],
        "whg": a["L0_attn_a_W_hg"].T,
        "win": a["L0_attn_b_W_in"],
        "wdt": a["L0_attn_b_W_dt"],
        "wout": a["L0_attn_b_W_out"],
        "wxp": np.concatenate([a["L0_attn_b_W_xproj"]] * 3, axis=1),
        "a_log": a["L0_attn_b_A_log"],
        "b_in": a["L0_attn_b_b_in"].reshape(2 * IK, P).T,
        "b_dt": a["L0_attn_b_b_dt"].reshape(IK, P).T,
        "b_xp": np.concatenate([a["L0_attn_b_b_xproj"]] * 3).reshape(96, 1),
        "dpar": a["L0_attn_b_D_param"].reshape(IK, P).T,
        "b_ff": np.concatenate([np.tile(a["L0_ffn_bias"], 2)[None, :]] * 96),
        "b_out": np.concatenate([np.tile(a["L0_attn_b_b_out"], 2)[None, :]] * 96),
        "wre": a["L0_ffn_w_freq_real"],
        "wim": a["L0_ffn_w_freq_imag"],
        "fcos": np.cos(phase).astype(np.float32),
        "fsin": np.sin(phase).astype(np.float32),
        "fnsin": (-np.sin(phase)).astype(np.float32),
        "ident": np.eye(P, dtype=np.float32),
        "sel": pick.astype(ml_dtypes.bfloat16),
        "part1": np.where(row >= 32, -1.0, 0.0).astype(np.float32),
        "part2": np.where(row >= 64, -1.0, 0.0).astype(np.float32),
    }
    arrays = {k: np.ascontiguousarray(v) for k, v in arrays.items()}
    nc = bacc.Bacc("TRN2", target_bir_lowering=False, num_devices=1)
    t = {k: nc.dram_tensor("in_" + k, v.shape, mybir.dt.from_np(v.dtype), kind="ExternalInput").ap() for k, v in arrays.items()}
    t["out"] = nc.dram_tensor("out_x", _OUT, F32, kind="ExternalOutput").ap()
    build(nc, t)
    r = run_bass_kernel_spmd(nc, [{"in_" + k: v for k, v in arrays.items()}], core_ids=[0])
    return r.results[0]["out_x"]
```

```python
import concourse.bass as bass
from concourse import mybir
from contextlib import ExitStack

F32 = mybir.dt.float32
BF16 = mybir.dt.bfloat16
ALU = mybir.AluOpType
ACT = mybir.ActivationFunctionType

BATCHES, SEQ, DM = 16, 512, 256
DI, DS = 512, 16
P = 128
TT = SEQ // P
DK = DM // P
IK = DI // P
JJ = 2
UNITS = IK // JJ * DS
RING, B_ROWS, C_ROWS = 4, 2, 4
AHEAD = 2
EPS = 1e-5

GATE_AT = {4: ["S0"], 11: ["A0", "R0a", "R0"], 13: ["T0", "T0a"], 14: ["G0", "G0a"], 15: ["H1"], 16: ["H1a"],
           17: ["H0", "G1"], 18: ["H0a", "G1a", "GS"], 19: ["CD", "C"], 21: ["Ca"], 23: ["X"], 24: ["Xa"],
           25: ["A1", "S1", "R1"], 26: ["T1", "T1a", "R1a"], 27: ["F0"], 29: ["F1", "F0a"], 31: ["F1a"]}
FEED_AT = {0: ["S2", "R2"], 1: ["A2", "R2a"], 2: ["T2", "T2a"], 3: ["U0", "U1", "Z2", "U0a"],
           4: ["Z1", "U1a", "Z2a", "Z1a"], 5: ["U3"], 6: ["U3a"], 7: ["U2", "Z3"], 8: ["U2a", "SU", "Z3a"],
           9: ["D1"], 10: ["D1a"], 11: ["D2"], 12: ["D2a"], 19: ["XP", "D3", "XPa", "D3a"], 21: ["D0"], 22: ["D0a"],
           24: ["SP"], 25: ["Z0", "V1"], 26: ["V2", "Z0a", "DD0"], 28: ["V2a"], 29: ["SZ"], 30: ["DD1"]}
CLOSE_AT = {0: ["YT"], 1: ["Y1"], 2: ["Y0", "Y1a", "Y0a", "Y1b"], 4: ["Y0b"], 25: ["W0", "W1"], 26: ["W0a"],
            27: ["A3", "W1a", "S3", "R3"], 28: ["T3", "T3a", "R3a"], 29: ["E1", "E0"], 30: ["E1a"], 31: ["E0a"]}
USES = {"T0": ["t00", "t01"], "T1": ["t10", "t11"], "T2": ["t20", "t21"], "T3": ["t30", "t31"],
        "X": ["x0", "x1"], "Y0": ["y0", "y1"], "Y1": ["y2", "y3"], "XP": ["xp"]}
USES.update({n: [n.lower()] for n in ("G0", "G1", "H0", "H1", "F0", "F1", "U0", "U1", "U2", "U3", "Z0", "Z1", "Z2", "Z3",
                                      "D0", "D1", "D2", "D3", "W0", "W1", "E0", "E1")})
LATE = ("C", "R1", "R2", "Y1b")
WIDE = (1, 0, 0, 1)
SETUP_AT = {e: next(k + late for k in GATE_AT if s in GATE_AT[k])
            for e, s, late in (("PE", "GS", 0), ("ACT", "GS", 1), ("DVE", "S1", 0), ("F0", "F0", 0), ("F1", "F1", 0))}
PEELED, LOOPED = 2, 12


class Batch:

    def __init__(self, r, c):
        self.r, self.c = r, c

    def count(self, per, more=0):
        n = per * self.c + more
        return n if self.r is None else self.r * (2 * per) + n

    def next(self, n=1):
        return Batch(self.r, self.c + n)

    @property
    def par(self):
        return self.c % 2


def row_at(k):
    return ("C", (k + 1) // 2) if k % 2 else None


FIRST_ROWS = [("C", DS)]


def parts_of(c):
    return [(table, ahead) for table, ahead in ((CLOSE_AT, -1), (FEED_AT, 1), (GATE_AT, 2)) if 0 <= c + ahead < BATCHES]


def steps_at(c, k):
    return [(s, ahead) for table, ahead in parts_of(c) for s in table.get(k, [])]


def uses_of(c):
    order = []
    for k in range(UNITS):
        if 0 <= c < BATCHES and k % 2 == 1 and (k + 1 < UNITS or c < BATCHES - 1):
            order.append(row_at(k))
        for s, _ in steps_at(c, k):
            order += USES.get(s, [])
    return order + (FIRST_ROWS if c == -1 else [])


STEADY = len(uses_of(1))


class Turns:

    def __init__(self, batch):
        self.batch = batch
        self.first = sum(len(uses_of(i)) for i in range(-2, batch.c))
        self.at = {key: self.first + n for n, key in enumerate(uses_of(batch.c))}

    def before(self, key):
        last = uses_of(self.batch.c - 1)
        self.at["before", key] = self.first - len(last) + last.index(key)
        return "before", key

    def row(self, which, s):
        return (which, s) if (which, s) in self.at else self.before((which, DS + s))

    def bank(self, key):
        return self.at[key] % 2

    def filled(self, key):
        return self.more(self.at[key] + 1, 2 * STEADY)

    def more(self, n, per):
        return n if self.batch.r is None else self.batch.r * per + n


def build(nc, t):
    ctx = ExitStack()
    with ctx:
        def sb(name, shape, dt=F32):
            return ctx.enter_context(nc.sbuf_tensor(name, shape, dt))

        def pb(name, shape):
            return ctx.enter_context(nc.psum_tensor(name, shape, F32))

        def sem(name):
            return ctx.enter_context(nc.semaphore(name))

        whg = sb("whg", [P, DK, 2 * DM])
        mix = sb("mix", [P, DK, DM])
        win = sb("win", [P, DK, 2 * DI])
        wdt = sb("wdt", [P, IK, DI])
        wout = sb("wout", [P, IK, DM])
        wxp = sb("wxp", [P, IK, 96])
        sel = sb("sel", [96, 2 * DS], BF16)
        ident = sb("ident", [P, P])
        decay = sb("decay", [P, IK, DS])
        b_in = sb("b_in", [P, 2 * IK])
        b_dt = sb("b_dt", [P, IK])
        b_xp = sb("b_xp", [96, 1])
        part1 = sb("part1", [96, 1])
        part2 = sb("part2", [96, 1])
        dpar = sb("dpar", [P, IK])
        bias_parts = [sb(f"bias_parts{i}", [96, 2 * DM], BF16) for i in range(2)]
        mhalf = sb("mhalf", [P, TT])
        xf = sb("xf", [P, TT, DM])
        xm = sb("xm", [P, TT, DM])
        xe = sb("xe", [P, TT, DM])
        xn = [sb(f"xn{i}", [P, TT, DM]) for i in range(2)]
        xnT = [sb(f"xnT{i}", [P, DK, SEQ]) for i in range(2)]
        stats = [sb(f"stats{i}", [P, TT, 6]) for i in range(4)]
        mv = [sb(f"mv{i}", [P, TT, 2]) for i in range(4)]
        rs = [sb(f"rs{i}", [P, TT]) for i in range(4)]
        nm = [sb(f"nm{i}", [P, TT]) for i in range(4)]
        keep = sb("keep", [P, DK, SEQ])
        take = sb("take", [P, DK, SEQ])
        cand = sb("cand", [P, DK, SEQ])
        u = [sb(f"u{i}", [P, IK, SEQ]) for i in range(2)]
        sz = [sb(f"sz{i}", [P, IK, SEQ]) for i in range(2)]
        dt = [sb(f"dt{i}", [P, IK, SEQ]) for i in range(2)]
        dtu = [sb(f"dtu{i}", [P, IK, SEQ]) for i in range(2)]
        xd = sb("xd", [96, SEQ])
        xhi = sb("xhi", [96, SEQ], BF16)
        xlo = sb("xlo", [96, SEQ])
        xmid = sb("xmid", [96, SEQ], BF16)
        parts = [sb(f"parts{i}", [96, SEQ], BF16) for i in range(2)]
        dec = sb("dec", [P, RING, JJ, SEQ])
        Cb = sb("Cb", [P, C_ROWS, SEQ])
        drive = sb("drive", [P, 2, JJ, SEQ])
        h = sb("h", [P, 2, JJ, SEQ])
        hc = sb("hc", [P, 2, JJ, SEQ])
        yT = sb("yT", [P, TT, DI])
        yg = sb("yg", [P, IK, SEQ])
        hpos = xn[1][:, :, :].rearrange("p i d -> p (i d)").rearrange("p (e n) -> p e n", e=DK)
        fcos, fsin, fnsin, wre = (u[1][:, i, :].rearrange("p (k n) -> p k n", k=DK) for i in range(4))
        wim = dt[1][:, 0, :].rearrange("p (k n) -> p k n", k=DK)
        specP = sz[1][:, 0, :].rearrange("p (k n) -> p k n", k=DK)
        specQ = sz[1][:, 1, :].rearrange("p (k n) -> p k n", k=DK)

        bias_rows = [dt[1][0:96, 1 + i, :] for i in range(2)]

        brow = [pb(f"brow{i}", [P, SEQ]) for i in range(B_ROWS)]
        yaccT = [pb(f"yaccT{i}", [P, DI]) for i in range(TT)]
        bank = [pb(f"bank{i}", [P, SEQ]) for i in range(2)]

        first_loaded, loaded = sem("first_loaded"), sem("loaded")
        consts = sem("consts")
        spec_full, spec_kept = sem("spec_full"), sem("spec_kept")
        mix_full, mix_kept = sem("mix_full"), sem("mix_kept")
        neg_exp, decay_ready = sem("neg_exp"), sem("decay_ready")
        filled = sem("filled")
        emptied = [sem("emptied0"), sem("emptied1")]
        x_in, spilled, back_in, stored = sem("x_in"), sem("spilled"), sem("back_in"), sem("stored")
        ln_stats, ln_mv, ln_var, ln_rs, ln_nm, ln_xn = (
            [sem(f"{n}{i}") for i in range(4)] for n in ("ln_stats", "ln_mv", "ln_var", "ln_rs", "ln_nm", "ln_xn"))
        gates, cand_sig, cand_sum, cand_in, state_a = (
            sem("gates"), sem("cand_sig"), sem("cand_sum"), sem("cand_in"), sem("state_a"))
        u_ready, sz_ready = sem("u_ready"), sem("sz_ready")
        bias_hi, bias_r1, bias_mid, bias_ready = sem("bias_hi"), sem("bias_r1"), sem("bias_mid"), sem("bias_ready")
        xd_ready, r1_ready, mid_ready, parts_ready = sem("xd_ready"), sem("r1_ready"), sem("mid_ready"), sem("parts_ready")
        soft_abs, soft_exp, soft_ln, dt_ready, dtu_ready = (
            sem("soft_abs"), sem("soft_exp"), sem("soft_ln"), sem("dt_ready"), sem("dtu_ready"))
        brow_ready = sem("brow_ready")
        decays, driven, scanned, weighed, summed = (
            sem("decays"), sem("driven"), sem("scanned"), sem("weighed"), sem("summed"))
        y_taken, y_gated = sem("y_taken"), sem("y_gated")

        def wait(eng, s, n):
            if not (isinstance(n, int) and n <= 0):
                eng.wait_ge(s, n)

        def wait_emptied(eng, tn, *keys, claim=None):
            for n in range(2):
                uses = [tn.at[key] // 2 + 1 for key in keys if tn.bank(key) == n]
                if claim is not None and tn.bank(claim) == n:
                    uses.append(tn.at[claim] // 2)
                if uses:
                    wait(eng, emptied[n], tn.more(max(uses), STEADY))

        LOADS = [
            (ident[:, :], t["ident"]),
            (whg[:, :, :], t["whg"].rearrange("(k p) n -> p k n", p=P)),
            (win[:, :, :], t["win"].rearrange("(k p) n -> p k n", p=P)),
            (wdt[:, :, :], t["wdt"].rearrange("(k p) n -> p k n", p=P)),
            (wout[:, :, :], t["wout"].rearrange("(k p) n -> p k n", p=P)),
            (wxp[:, :, :], t["wxp"].rearrange("(k p) n -> p k n", p=P)),
            (sel[:, :], t["sel"]),
            (decay[:, :, :], t["a_log"].rearrange("(k p) n -> p k n", p=P)),
            (b_in[:, :], t["b_in"]), (b_dt[:, :], t["b_dt"]), (b_xp[:, :], t["b_xp"]),
            (part1[:, :], t["part1"]), (part2[:, :], t["part2"]), (dpar[:, :], t["dpar"]),
            (bias_rows[0], t["b_ff"]), (bias_rows[1], t["b_out"]),
            (fcos, t["fcos"].rearrange("(k p) n -> p k n", p=P)),
            (fsin, t["fsin"].rearrange("(k p) n -> p k n", p=P)),
            (fnsin, t["fnsin"].rearrange("(k p) n -> p k n", p=P)),
            (wre, t["wre"].rearrange("(k p) n -> p k n", p=P)),
            (wim, t["wim"].rearrange("(k p) n -> p k n", p=P)),
        ]
        FIRST_LOADS = 2
        all_loaded = 16 * (len(LOADS) - FIRST_LOADS)

        block = ctx.enter_context(nc.Block())

        @block.sync
        def _(sp):
            spill = [t["spill"][c].rearrange("(i p) d -> p i d", p=P) for c in range(BATCHES)]

            def load_x(b):
                if b.c > 0:
                    sp.wait_ge(ln_xn[1], b.count(1))
                    wait_emptied(sp, Turns(b.next(-3)), "f0", "f1")
                sp.dma_start(xf[:, :, :], t["x"][b.c].rearrange("(i p) d -> p i d", p=P)).then_inc(x_in, 16)

            def spill_residual(b):
                wait_emptied(sp, Turns(b.next(-2)), "f0", "f1")
                sp.dma_start(spill[b.c], xm[:, :, :]).then_inc(spilled, 16)

            def load_residual(b):
                sp.wait_ge(spilled, b.count(16, 16))
                wait(sp, stored, b.count(16))
                sp.dma_start(xe[:, :, :], spill[b.c]).then_inc(back_in, 16)

            def store(b):
                wait_emptied(sp, Turns(b.next()), "e0", "e1")
                sp.dma_start(t["out"][b.c].rearrange("(i p) d -> p i d", p=P), xe[:, :, :]).then_inc(stored, 16)

            load_x(Batch(None, 0))
            for n, (dst, src) in enumerate(LOADS):
                sp.dma_start(dst, src).then_inc(first_loaded if n < FIRST_LOADS else loaded, 16)
            for c in range(-2, BATCHES + 1):
                if c > 0:
                    load_residual(Batch(None, c - 1))
                if c + 2 < BATCHES:
                    spill_residual(Batch(None, c + 2))
                if c + 3 < BATCHES:
                    load_x(Batch(None, c + 3))
                if c > 0:
                    store(Batch(None, c - 1))
            sp.wait_ge(stored, 16 * BATCHES)

        def spans(eng, span):
            def alone(first, end):
                for c in range(first, end):
                    span(Batch(None, c), Turns(Batch(None, c)))

            alone(-2, PEELED)
            with eng.Fori(0, LOOPED // 2, 1) as r:
                for c in (PEELED, PEELED + 1):
                    span(Batch(r, c), Turns(Batch(r, c)))
            alone(PEELED + LOOPED, BATCHES + 1)

        def scans(b):
            return 0 <= b.c < BATCHES

        def scans_unit(b, k):
            return 0 <= b.c + k // UNITS < BATCHES

        def steps(step, b, k, tn, only=lambda s: True):
            for s, ahead in steps_at(b.c, k):
                if only(s):
                    step(s, b.next(ahead), tn)

        def wait_row(eng, tn, which, s):
            wait_emptied(eng, tn, tn.row(which, s))

        @block.scalar
        def _(act):
            def setup():
                act.wait_ge(loaded, all_loaded)
                act.activation(decay[:, :, :], decay[:, :, :], ACT.Exp).then_inc(neg_exp, 1)
                act.wait_ge(neg_exp, 1)
                act.activation(decay[:, :, :], decay[:, :, :], ACT.Copy, scale=-1.0).then_inc(decay_ready, 1)
                act.wait_ge(spec_full, 1)
                act.activation(specP, yaccT[0][:, :].rearrange("p (k n) -> p k n", k=DK), ACT.Copy).then_inc(spec_kept, 1)
                act.wait_ge(spec_full, 2)
                act.activation(specQ, yaccT[1][:, :].rearrange("p (k n) -> p k n", k=DK), ACT.Copy).then_inc(spec_kept, 1)
                act.wait_ge(mix_full, 1)
                act.activation(mix[:, :, :], brow[0][:, :].rearrange("p (k n) -> p k n", k=DK), ACT.Copy,
                               scale=1.0 / DM).then_inc(mix_kept, 1)
                act.wait_ge(decay_ready, 1)
                for i in range(2):
                    wait(act, bias_ready, i)
                    act.activation(xhi[:, :], bias_rows[i], ACT.Copy).then_inc(bias_hi, 1)
                    act.wait_ge(bias_r1, i + 1)
                    act.activation(xmid[:, :], xlo[:, :], ACT.Copy).then_inc(bias_mid, 1)
                act.wait_ge(bias_ready, 2)

            def norm_rows(n, src, b):
                act.wait_ge(ln_nm[n], b.count(1, 1))
                for i in range(TT):
                    last = act.activation(xn[WIDE[n]][:, i, :], src[:, i, :], ACT.Identity,
                                          scale=rs[n][:, i:i + 1], bias=nm[n][:, i:i + 1])
                last.then_inc(ln_xn[n], 1)

            def keep_transpose(n, tn):
                for k in range(DK):
                    key = f"t{n}{k}"
                    act.wait_ge(filled, tn.filled(key))
                    act.activation(xnT[WIDE[n]][:, k, :], bank[tn.bank(key)][:, :], ACT.Copy).then_inc(emptied[tn.bank(key)], 1)

            def step(s, b, tn):
                q = b.par
                made = s[0:-1].lower()
                if s in ("A0", "A1"):
                    norm_rows(int(s[1]), xf, b)
                elif s == "A2":
                    norm_rows(2, xm, b)
                elif s == "A3":
                    act.wait_ge(cand_sum, b.count(1, 4) if b.r is not None else min(b.c + 4, BATCHES))
                    norm_rows(3, xe, b)
                elif s in ("T0a", "T1a", "T2a", "T3a"):
                    keep_transpose(int(s[1]), tn)
                elif s in ("G0a", "G1a"):
                    e, n = int(s[1]), tn.bank(made)
                    act.wait_ge(filled, tn.filled(made))
                    act.activation(take[:, e, :], bank[n][:, :], ACT.Copy).then_inc(emptied[n], 1)
                elif s in ("H0a", "H1a"):
                    e, n = int(s[1]), tn.bank(made)
                    act.wait_ge(filled, tn.filled(made))
                    act.activation(cand[:, e, :], bank[n][:, :], ACT.Relu, scale=-1.0)
                    act.activation(hpos[:, e, :], bank[n][:, :], ACT.Relu).then_inc(emptied[n], 1)
                elif s == "GS":
                    wait_emptied(act, tn, "g0", "g1", "h0", "h1")
                    act.activation(cand[:, :, :], cand[:, :, :], ACT.Sigmoid, scale=-1.0).then_inc(cand_sig, 1)
                    act.activation(keep[:, :, :], take[:, :, :], ACT.Sigmoid, scale=-1.0).then_inc(gates, 1)
                    act.wait_ge(gates, b.count(2, 1))
                    act.activation(take[:, :, :], take[:, :, :], ACT.Sigmoid).then_inc(gates, 1)
                elif s[0] in "UZ" and s[-1] == "a":
                    m = int(s[1])
                    dst, at = (u[q], m) if s[0] == "U" else (sz[q], IK + m)
                    if s[0] == "U" and "y3" in tn.at:
                        wait_emptied(act, tn, "y2", "y3")
                    if s[0] == "Z":
                        wait(act, y_gated, b.count(2, -2))
                    act.wait_ge(filled, tn.filled(made))
                    act.activation(dst[:, m, :], bank[tn.bank(made)][:, :], ACT.Identity, bias=b_in[:, at:at + 1])\
                       .then_inc(emptied[tn.bank(made)], 1)
                elif s == "SU":
                    wait_emptied(act, tn, "u0", "u1", "u2", "u3")
                    act.activation(u[q][:, :, :], u[q][:, :, :], ACT.Silu).then_inc(u_ready, 1)
                elif s == "SZ":
                    wait_emptied(act, tn, "z0", "z1", "z2", "z3")
                    act.activation(sz[q][:, :, :], sz[q][:, :, :], ACT.Silu).then_inc(sz_ready, 1)
                elif s == "XPa":
                    key = "xp"
                    act.wait_ge(filled, tn.filled(key))
                    act.activation(xd[:, :], bank[tn.bank(key)][0:96, :], ACT.Identity, bias=b_xp[:, :]).then_inc(xd_ready, 1)
                    act.activation(xhi[:, :], bank[tn.bank(key)][0:96, :], ACT.Identity, bias=b_xp[:, :])\
                       .then_inc(emptied[tn.bank(key)], 1)
                elif s == "V2":
                    act.wait_ge(r1_ready, b.count(1, 1))
                    act.activation(xmid[:, :], xlo[:, :], ACT.Copy).then_inc(mid_ready, 1)
                elif s in ("D0a", "D1a", "D2a", "D3a"):
                    m, key = int(s[1]), made
                    act.wait_ge(filled, tn.filled(key))
                    act.activation(dtu[q][:, m, :], bank[tn.bank(key)][:, :], ACT.Abs, bias=b_dt[:, m:m + 1])\
                       .then_inc(soft_abs, 1)
                    act.activation(dt[q][:, m, :], bank[tn.bank(key)][:, :], ACT.Relu, bias=b_dt[:, m:m + 1])\
                       .then_inc(emptied[tn.bank(key)], 1)
                elif s == "SP":
                    v = dtu[q][:, :, :]
                    act.wait_ge(soft_abs, b.count(IK, IK))
                    act.activation(v, v, ACT.Exp, scale=-1.0).then_inc(soft_exp, 1)
                    act.wait_ge(soft_exp, b.count(1, 1))
                    act.activation(v, v, ACT.Ln, bias=1.0).then_inc(soft_ln, 1)
                elif s == "YT":
                    act.wait_ge(summed, b.count(UNITS, UNITS))
                    for i in range(TT):
                        act.activation(yT[:, i, :], yaccT[i][:, :], ACT.Copy).then_inc(y_taken, 1)

            def copy_row(b, key, tn):
                row, n = key[1], tn.bank(key)
                act.wait_ge(filled, tn.filled(key))
                wait(act, weighed, b.count(UNITS, (row - C_ROWS + 1) * (UNITS // DS)))
                act.activation(Cb[:, row % C_ROWS, :], bank[n][:, :], ACT.Copy).then_inc(emptied[n], 1)

            def decay_unit(b, k):
                b, k = (b.next(), k - UNITS) if k >= UNITS else (b, k)
                if k < JJ:
                    act.wait_ge(dt_ready, b.count(2, k + 1))
                wait(act, scanned, b.count(UNITS, k - RING + 1))
                for jj in range(JJ):
                    s, j = k // JJ, k % JJ * JJ + jj
                    last = act.activation(dec[:, k % RING, jj, 1:SEQ], dt[b.par][:, j, 1:SEQ], ACT.Exp,
                                          scale=decay[:, j, s:s + 1])
                last.then_inc(decays, 1)

            def span(b, tn):
                for k in range(UNITS):
                    if b.c == -2 and k == SETUP_AT["ACT"]:
                        setup()
                    if row_at(k) in tn.at and scans(b):
                        copy_row(b, row_at(k), tn)
                    if scans(b) and scans_unit(b, k + AHEAD):
                        decay_unit(b, k + AHEAD)
                    steps(step, b, k, tn)
                if b.c == -1:
                    for key in FIRST_ROWS:
                        copy_row(b, key, tn)
                    for k in range(AHEAD):
                        decay_unit(b, UNITS + k)

            spans(act, span)

        @block.vector
        def _(dve):
            dve.memset(dec[:, :, :, 0:1], 0.0).then_inc(consts, 1)
            dve.memset(mhalf[:, :], -0.5).then_inc(consts, 1)
            def setup():
                dve.wait_ge(loaded, all_loaded)
                dve.wait_ge(consts, 2)
                for i in range(2):
                    dve.wait_ge(bias_hi, i + 1)
                    dve.scalar_tensor_tensor(xlo[:, :], xhi[:, :], part1[:, :], bias_rows[i], ALU.mult, ALU.add).then_inc(bias_r1, 1)
                    dve.wait_ge(bias_mid, i + 1)
                    dve.scalar_tensor_tensor(bias_parts[i][:, :], xmid[:, :], part2[:, :], xlo[:, :], ALU.mult, ALU.add)\
                       .then_inc(bias_ready, 1)

            def norm_stats(n, src, b):
                for i in range(TT):
                    last = dve.bn_stats(stats[n][:, i, :], src[:, i, :])
                last.then_inc(ln_stats[n], 1)
                dve.drain()
                for i in range(TT):
                    last = dve.bn_aggr(mv[n][:, i, :], stats[n][:, i, :])
                last.then_inc(ln_mv[n], 1)
                dve.wait_ge(ln_mv[n], b.count(1, 1))
                dve.tensor_scalar(rs[n][:, :], mv[n][:, :, 1], 1.0, EPS, ALU.mult, ALU.add).then_inc(ln_var[n], 1)

            def add_rows(dst, src, key, tn):
                n, i = tn.bank(key), int(key[1])
                at = slice(2 * i, 2 * i + 2)
                dve.wait_ge(filled, tn.filled(key))
                dve.tensor_tensor(dst[:, at, :], src[:, at, :], bank[n][:, :].rearrange("p (i d) -> p i d", i=2), ALU.add)\
                   .then_inc(emptied[n], 1)

            def step(s, b, tn):
                if s == "S0":
                    dve.wait_ge(x_in, b.count(16, 16))
                    norm_stats(0, xf, b)
                elif s == "S1":
                    wait_emptied(dve, tn, "x0", "x1")
                    norm_stats(1, xf, b)
                elif s == "S2":
                    wait_emptied(dve, tn, tn.before("f0"), tn.before("f1"))
                    norm_stats(2, xm, b)
                elif s == "S3":
                    wait_emptied(dve, tn, "w0", "w1")
                    norm_stats(3, xe, b)
                elif s in ("R0a", "R1a", "R2a", "R3a"):
                    n = int(s[1])
                    dve.wait_ge(ln_rs[n], b.count(1, 1))
                    dve.scalar_tensor_tensor(nm[n][:, :], mv[n][:, :, 0], -1.0, rs[n][:, :], ALU.mult, ALU.mult)\
                       .then_inc(ln_nm[n], 1)
                elif s == "CD":
                    dve.wait_ge(cand_sig, b.count(1, 1))
                    wait_emptied(dve, tn, "h0", "h1")
                    dve.tensor_tensor(cand[:, :, :], hpos, cand[:, :, :], ALU.add).then_inc(cand_sum, 1)
                elif s == "Ca":
                    for e in range(DK):
                        dve.wait_ge(cand_in, b.count(DK, e + 1))
                        dve.tensor_tensor_scan(cand[:, e, :], keep[:, e, :], take[:, e, :], 0.0,
                                               ALU.mult, ALU.add).then_inc(state_a, 1)
                elif s == "Xa":
                    for e in range(DK):
                        n = tn.bank(f"x{e}")
                        d = xf[:, :, e * P:(e + 1) * P]
                        dve.wait_ge(filled, tn.filled(f"x{e}"))
                        if e == 0:
                            dve.wait_ge(ln_xn[0], b.count(1, 1))
                        dve.tensor_tensor(d, d, bank[n][:, :].rearrange("p (i d) -> p i d", i=TT), ALU.add)\
                           .then_inc(emptied[n], 1)
                elif s in ("F0a", "F1a"):
                    wait(dve, ln_xn[2], b.count(1))
                    wait(dve, spilled, b.count(16))
                    add_rows(xm, xf, "f" + s[1], tn)
                elif s == "V1":
                    dve.wait_ge(xd_ready, b.count(1, 1))
                    wait_emptied(dve, tn, "xp")
                    dve.scalar_tensor_tensor(xlo[:, :], xhi[:, :], part1[:, :], xd[:, :], ALU.mult, ALU.add)\
                       .then_inc(r1_ready, 1)
                elif s == "V2a":
                    dve.wait_ge(mid_ready, b.count(1, 1))
                    dve.scalar_tensor_tensor(parts[b.par][:, :], xmid[:, :], part2[:, :], xlo[:, :], ALU.mult, ALU.add)\
                       .then_inc(parts_ready, 1)
                elif s in ("Y0a", "Y1a"):
                    for j in (2 * int(s[1]), 2 * int(s[1]) + 1):
                        n = tn.bank(f"y{j}")
                        dve.wait_ge(filled, tn.filled(f"y{j}"))
                        dve.scalar_tensor_tensor(yg[:, j, :], u[b.par][:, j, :], dpar[:, j:j + 1], bank[n][:, :],
                                                 ALU.mult, ALU.add).then_inc(emptied[n], 1)
                elif s in ("W0a", "W1a"):
                    dve.wait_ge(back_in, b.count(16, 16))
                    add_rows(xe, xe, s[0:2].lower(), tn)
                elif s in ("E0a", "E1a"):
                    dve.wait_ge(ln_xn[3], b.count(1, 1))
                    add_rows(xe, xe, s[0:2].lower(), tn)

            def drive_unit(b, k):
                b, k = (b.next(), k - UNITS) if k >= UNITS else (b, k)
                dve.wait_ge(brow_ready, b.count(DS, k // JJ + 1))
                if k < JJ:
                    dve.wait_ge(dtu_ready, b.count(2, k + 1))
                wait(dve, scanned, b.count(UNITS, k - 1))
                j = k % JJ * JJ
                row = brow[k // JJ % B_ROWS][:, :].rearrange("p (o n) -> p o n", o=1)
                dve.tensor_tensor(drive[:, k % 2, :, :], dtu[b.par][:, j:j + JJ, :], row.broadcast_to((P, JJ, SEQ)), ALU.mult)\
                   .then_inc(driven, 1)

            def scan_unit(b, k):
                dve.wait_ge(decays, b.count(UNITS, k + 1))
                wait(dve, weighed, b.count(UNITS, k - 1))
                dve.wait_ge(driven, b.count(UNITS, k + 1))
                dve.tensor_tensor_scan(h[:, k % 2, :, :].rearrange("p j n -> p (j n)"),
                                       dec[:, k % RING, :, :].rearrange("p j n -> p (j n)"),
                                       drive[:, k % 2, :, :].rearrange("p j n -> p (j n)"), 0.0, ALU.mult, ALU.add)\
                   .then_inc(scanned, 1)

            def span(b, tn):
                for k in range(UNITS):
                    if b.c == -2 and k == SETUP_AT["DVE"]:
                        setup()
                    if scans(b):
                        if scans_unit(b, k + 1):
                            drive_unit(b, k + 1)
                        scan_unit(b, k)
                    steps(step, b, k, tn)
                if b.c == -1:
                    drive_unit(b, UNITS)

            spans(dve, span)

        @block.gpsimd
        def _(pool):
            pool.wait_ge(consts, 2)

            def step(s, b, tn):
                q = b.par
                if s in ("R0", "R1", "R2", "R3"):
                    n = int(s[1])
                    pool.wait_ge(ln_var[n], b.count(1, 1))
                    pool.tensor_tensor(rs[n][:, :], rs[n][:, :], mhalf[:, :], ALU.pow).then_inc(ln_rs[n], 1)
                elif s == "C":
                    for e in range(DK):
                        pool.wait_ge(gates, b.count(2, 2))
                        pool.wait_ge(cand_sum, b.count(1, 1))
                        pool.tensor_tensor(take[:, e, :], take[:, e, :], cand[:, e, :], ALU.mult).then_inc(cand_in, 1)
                elif s in ("DD0", "DD1"):
                    half = int(s[2])
                    at = slice(JJ * half, JJ * half + JJ)
                    pool.wait_ge(soft_ln, b.count(1, 1))
                    wait_emptied(pool, tn, f"d{JJ * half}", f"d{JJ * half + 1}")
                    pool.tensor_tensor(dt[q][:, at, :], dt[q][:, at, :], dtu[q][:, at, :], ALU.add).then_inc(dt_ready, 1)
                    pool.wait_ge(dt_ready, b.count(2, half + 1))
                    pool.wait_ge(u_ready, b.count(1, 1))
                    pool.tensor_tensor(dtu[q][:, at, :], dt[q][:, at, :], u[q][:, at, :], ALU.mult).then_inc(dtu_ready, 1)
                elif s in ("Y0b", "Y1b"):
                    half = int(s[1])
                    at = slice(JJ * half, JJ * half + JJ)
                    wait_emptied(pool, tn, f"y{JJ * half}", f"y{JJ * half + 1}")
                    pool.wait_ge(sz_ready, b.count(1, 1))
                    pool.tensor_tensor(yg[:, at, :], yg[:, at, :], sz[q][:, at, :], ALU.mult).then_inc(y_gated, 1)

            def weigh_unit(b, k, tn):
                pool.wait_ge(scanned, b.count(UNITS, k + 1))
                s = k // JJ
                wait_row(pool, tn, "C", s)
                wait(pool, summed, b.count(UNITS, k - 1))
                pool.tensor_tensor(hc[:, k % 2, :, :], h[:, k % 2, :, :],
                                   Cb[:, s % C_ROWS:s % C_ROWS + 1, :].broadcast_to((P, JJ, SEQ)), ALU.mult)\
                    .then_inc(weighed, 1)

            def span(b, tn):
                for k in range(UNITS):
                    steps(step, b, k, tn, lambda s: s not in LATE)
                    if scans(b):
                        weigh_unit(b, k, tn)
                    steps(step, b, k, tn, lambda s: s in LATE)

            spans(pool, span)

        @block.tensor
        def _(pe):
            pe.wait_ge(first_loaded, 16 * FIRST_LOADS)

            def pick(row):
                return sel[:, row:row + 1].broadcast_to((96, P))

            def mm(out, lhsT, rhs, first, last):
                return pe.matmul(out, lhsT, rhs, start=first, stop=last)

            def setup():
                pe.wait_ge(loaded, all_loaded)
                for half, (first, second) in enumerate((((wre, fcos), (wim, fsin)), ((wim, fcos), (wre, fnsin)))):
                    for n in range(DK):
                        out = yaccT[half][:, n * DM:(n + 1) * DM]
                        for i, (w, f) in enumerate((first, second)):
                            for k in range(DK):
                                last = mm(out, w[:, k, n * P:(n + 1) * P], f[:, k, :], i == 0 and k == 0, i == 1 and k == DK - 1)
                    last.then_inc(spec_full, 1)
                pe.wait_ge(spec_kept, 2)
                for j in range(DK):
                    out = brow[0][:, j * DM:(j + 1) * DM]
                    for i, (s, f) in enumerate(((specP, fcos), (specQ, fnsin))):
                        for k in range(DK):
                            last = mm(out, s[:, k, j * P:(j + 1) * P], f[:, k, :], i == 0 and k == 0, i == 1 and k == DK - 1)
                last.then_inc(mix_full, 1)

            def claim(tn, key, *after):
                wait_emptied(pe, tn, *after, claim=key)
                return bank[tn.bank(key)]

            def transpose_rows(n, b, tn):
                pe.wait_ge(ln_xn[n], b.count(1, 1))
                for k in range(DK):
                    out = claim(tn, f"t{n}{k}")
                    for i in range(TT):
                        last = pe.transpose(out[:, i * P:(i + 1) * P], xn[WIDE[n]][:, i, k * P:(k + 1) * P], ident[:, :])
                    last.then_inc(filled, 1)

            def project(tn, key, weight, moving, n=P, after=()):
                out = claim(tn, key, *after)
                for k, (w, m) in enumerate(zip(weight, moving)):
                    last = mm(out[0:n, :], w, m, k == 0, k == len(weight) - 1)
                last.then_inc(filled, 1)

            def rows_out(tn, key, source, weight, blocks, bias, after=()):
                out = claim(tn, key, *after)
                mm(out[:, :], pick(0), bias[:, :], True, False)
                for ii in range(2):
                    i = 2 * int(key[1]) + ii
                    for k in range(blocks):
                        last = mm(out[:, ii * DM:(ii + 1) * DM], source[:, k, i * P:(i + 1) * P], weight[:, k, :],
                                  False, ii == 1 and k == blocks - 1)
                last.then_inc(filled, 1)

            def step(s, b, tn):
                q = b.par
                if s in ("T0", "T1", "T2", "T3"):
                    transpose_rows(int(s[1]), b, tn)
                elif s in ("G0", "G1", "H0", "H1"):
                    at = (DM if s[0] == "G" else 0) + int(s[1]) * P
                    project(tn, s.lower(), [whg[:, k, at:at + P] for k in range(DK)],
                            [xnT[WIDE[0]][:, k, :] for k in range(DK)], after=("t00", "t01"))
                elif s == "X":
                    for e in range(DK):
                        pe.wait_ge(state_a, b.count(DK, e + 1))
                        out = claim(tn, f"x{e}")
                        for i in range(TT):
                            last = pe.transpose(out[:, i * P:(i + 1) * P], cand[:, e, i * P:(i + 1) * P], ident[:, :])
                        last.then_inc(filled, 1)
                elif s in ("F0", "F1"):
                    rows_out(tn, s.lower(), xnT[WIDE[1]], mix, DK, bias_parts[0], after=("t10", "t11"))
                elif s in ("U0", "U1", "U2", "U3", "Z0", "Z1", "Z2", "Z3"):
                    at = (0 if s[0] == "U" else DI) + int(s[1]) * P
                    project(tn, s.lower(), [win[:, k, at:at + P] for k in range(DK)],
                            [xnT[WIDE[2]][:, k, :] for k in range(DK)], after=("t20", "t21"))
                elif s == "XP":
                    pe.wait_ge(u_ready, b.count(1, 1))
                    project(tn, "xp", [wxp[:, k, :] for k in range(IK)], [u[q][:, k, :] for k in range(IK)], 96)
                elif s in ("D0", "D1", "D2", "D3"):
                    m = int(s[1])
                    pe.wait_ge(u_ready, b.count(1, 1))
                    project(tn, s.lower(), [wdt[:, k, m * P:(m + 1) * P] for k in range(IK)],
                            [u[q][:, k, :] for k in range(IK)])
                elif s in ("Y0", "Y1"):
                    pe.wait_ge(y_taken, b.count(TT, TT))
                    for j in (2 * int(s[1]), 2 * int(s[1]) + 1):
                        out = claim(tn, f"y{j}")
                        for i in range(TT):
                            last = pe.transpose(out[:, i * P:(i + 1) * P], yT[:, i, j * P:(j + 1) * P], ident[:, :])
                        last.then_inc(filled, 1)
                elif s in ("W0", "W1"):
                    pe.wait_ge(y_gated, b.count(2, 2))
                    rows_out(tn, s.lower(), yg, wout, IK, bias_parts[1])
                elif s in ("E0", "E1"):
                    rows_out(tn, s.lower(), xnT[WIDE[3]], mix, DK, bias_parts[0], after=("t30", "t31"))

            def send_c(b, key, tn):
                src = b.next(key[1] // DS)
                if key[1] >= DS:
                    pe.wait_ge(parts_ready, src.count(1, 1))
                out = claim(tn, key)
                mm(out[:, :], pick(DS + key[1] % DS), parts[src.par][:, :], True, True).then_inc(filled, 1)

            def send_b(b, row):
                src = b.next(row // DS)
                if row >= DS:
                    pe.wait_ge(parts_ready, src.count(1, 1))
                wait(pe, driven, b.count(UNITS, (row - B_ROWS + 1) * (UNITS // DS)))
                mm(brow[row % B_ROWS][:, :], pick(row % DS), parts[src.par][:, :], True, True).then_inc(brow_ready, 1)

            def sum_unit(b, k):
                pe.wait_ge(weighed, b.count(UNITS, k + 1))
                if k == 0:
                    wait(pe, y_taken, b.count(TT, 0))
                for jj in range(JJ):
                    j = k % JJ * JJ + jj
                    for i in range(TT):
                        last = pe.matmul(yaccT[i][:, j * P:(j + 1) * P], hc[:, k % 2, jj, i * P:(i + 1) * P], ident[:, :],
                                         start=k == 0 and jj == 0, stop=k == UNITS - 1 and jj == JJ - 1,
                                         is_transpose=True, skip_group_check=True)
                last.then_inc(summed, 1)

            def span(b, tn):
                for k in range(UNITS):
                    if b.c == -2 and k == SETUP_AT["PE"]:
                        setup()
                    if b.c == -2 and k == min(SETUP_AT["F0"], SETUP_AT["F1"]):
                        pe.wait_ge(mix_kept, 1)
                        pe.wait_ge(bias_ready, 2)
                    if row_at(k) in tn.at and scans(b):
                        send_c(b, row_at(k), tn)
                    if k % 2 == 1 and scans(b) and scans_unit(b, k + 3):
                        send_b(b, (k + 3) // 2)
                    if scans_unit(b, k - 1):
                        sum_unit(*((b, k - 1) if k > 0 else (b.next(-1), UNITS - 1)))
                    steps(step, b, k, tn)
                if b.c == -1:
                    send_b(b, DS)
                    send_b(b, DS + 1)
                    for key in FIRST_ROWS:
                        send_c(b, key, tn)

            spans(pe, span)


_OUT = (BATCHES, SEQ, DM)


def kernel(**inputs):
    import numpy as np
    import ml_dtypes
    import concourse.bacc as bacc
    from concourse.bass_utils import run_bass_kernel_spmd

    a = {k: np.asarray(v) for k, v in inputs.items()}
    phase = 2.0 * np.pi * (np.outer(np.arange(DM), np.arange(DM)) % DM) / DM
    pick = np.concatenate([np.eye(2 * DS, dtype=np.float32)] * 3)
    row = np.arange(96)[:, None]
    arrays = {
        "x": a["L0_attn_a_x"],
        "whg": a["L0_attn_a_W_hg"].T,
        "win": a["L0_attn_b_W_in"],
        "wdt": a["L0_attn_b_W_dt"],
        "wout": a["L0_attn_b_W_out"],
        "wxp": np.concatenate([a["L0_attn_b_W_xproj"]] * 3, axis=1),
        "a_log": a["L0_attn_b_A_log"],
        "b_in": a["L0_attn_b_b_in"].reshape(2 * IK, P).T,
        "b_dt": a["L0_attn_b_b_dt"].reshape(IK, P).T,
        "b_xp": np.concatenate([a["L0_attn_b_b_xproj"]] * 3).reshape(96, 1),
        "dpar": a["L0_attn_b_D_param"].reshape(IK, P).T,
        "b_ff": np.concatenate([np.tile(a["L0_ffn_bias"], 2)[None, :]] * 96),
        "b_out": np.concatenate([np.tile(a["L0_attn_b_b_out"], 2)[None, :]] * 96),
        "wre": a["L0_ffn_w_freq_real"],
        "wim": a["L0_ffn_w_freq_imag"],
        "fcos": np.cos(phase).astype(np.float32),
        "fsin": np.sin(phase).astype(np.float32),
        "fnsin": (-np.sin(phase)).astype(np.float32),
        "ident": np.eye(P, dtype=np.float32),
        "sel": pick.astype(ml_dtypes.bfloat16),
        "part1": np.where(row >= 32, -1.0, 0.0).astype(np.float32),
        "part2": np.where(row >= 64, -1.0, 0.0).astype(np.float32),
    }
    arrays = {k: np.ascontiguousarray(v) for k, v in arrays.items()}
    nc = bacc.Bacc("TRN2", target_bir_lowering=False, num_devices=1)
    t = {k: nc.dram_tensor("in_" + k, v.shape, mybir.dt.from_np(v.dtype), kind="ExternalInput").ap() for k, v in arrays.items()}
    t["spill"] = nc.dram_tensor("spill", _OUT, F32, kind="Internal").ap()
    t["out"] = nc.dram_tensor("out_x", _OUT, F32, kind="ExternalOutput").ap()
    build(nc, t)
    r = run_bass_kernel_spmd(nc, [{"in_" + k: v for k, v in arrays.items()}], core_ids=[0])
    return r.results[0]["out_x"]
```
